# Optimizing a Trainium2 kernel written in Bass

```python
import numpy as np
import jax
import jax.numpy as jnp

def _softmax(x, axis=-1):
    return jax.nn.softmax(x, axis=axis)

def _gelu(x):
    return jax.nn.gelu(x, approximate=True)

def _silu(x):
    return jax.nn.silu(x)

def _sigmoid(x):
    return jax.nn.sigmoid(x)

def _layernorm(x, axis=-1, eps=1e-05):
    m = jnp.mean(x, axis=axis, keepdims=True)
    v = jnp.var(x, axis=axis, keepdims=True)
    return (x - m) / jnp.sqrt(v + eps)

def _scatter_add(tgt, idx, src, axis=0):
    return tgt.at[idx].add(src)

def _segment_sum(src, seg, n):
    return jax.ops.segment_sum(src, seg, n)
kernel_name = 'mk_flamingo_gated_d1_seqx_r8_492b33'

def setup_inputs(seed: int=0):
    np.random.seed(seed)
    _w = jnp.asarray

    def _rec_inputs():
        import jax
        import jax.numpy as jnp
        _rk = jax.random.key(seed)
        x = 7.22e-05 + 1 * jax.random.normal(jax.random.fold_in(_rk, 1), (16, 100, 128), jnp.float32)
        _lenS = 100 - jax.random.randint(jax.random.fold_in(_rk, 7), (16,), 0, max(1, 100 // 4) + 1, jnp.int32)
        _lenS2 = 1444 - jax.random.randint(jax.random.fold_in(_rk, 8), (16,), 0, max(1, 1444 // 4) + 1, jnp.int32)
        _ctx_768P = jax.random.normal(jax.random.fold_in(_rk, 11), (16, 16, 96), jnp.float32)
        _ctx_768c = jax.random.dirichlet(jax.random.fold_in(_rk, 511), 0.3 * jnp.ones((16,), jnp.float32), (16, 1444))
        _ctx_768t = jnp.einsum('bsk,bkd->bsd', _ctx_768c, _ctx_768P)
        _ctx_768t = _ctx_768t * jax.lax.rsqrt(jnp.mean(jnp.square(_ctx_768t)) + 1e-12) * 0.953939
        ctx_768 = -0.000191848 + 0.999787 * (_ctx_768t + 0.3 * jax.random.normal(jax.random.fold_in(_rk, 611), (16, 1444, 96), jnp.float32))
        _g = jax.random.normal(jax.random.fold_in(_rk, 9001), (2, 1), jnp.float32)
        _g = jnp.sign(_g) * jnp.maximum(jnp.abs(_g), 1.0) + (_g == 0) * 1.0
        g_xattn = _g[0]
        g_ffn = _g[1]
        return (x, ctx_768, g_xattn, g_ffn)
    x, ctx_768, g_xattn, g_ffn = _rec_inputs()

    def _L0_xattn_setup():
        import jax, jax.numpy as jnp
        import numpy as np
        HEADS = 16
        DIM_HEAD = 64
        QUERY_DIM = 128
        CONTEXT_DIM = 96
        INNER = HEADS * DIM_HEAD
        SCALE = DIM_HEAD ** (-0.5)
        key = jax.random.key(seed)
        ks = jax.random.split(key, 7)
        B, Sq, Skv = (4, 256, 256)
        x = jax.random.normal(ks[0], (B, Sq, QUERY_DIM), dtype=jnp.float32)
        context = jax.random.normal(ks[1], (B, Skv, CONTEXT_DIM), dtype=jnp.float32)
        w_q = jax.random.normal(ks[2], (QUERY_DIM, INNER), dtype=jnp.float32) / np.sqrt(QUERY_DIM)
        w_k = jax.random.normal(ks[3], (CONTEXT_DIM, INNER), dtype=jnp.float32) / np.sqrt(CONTEXT_DIM)
        w_v = jax.random.normal(ks[4], (CONTEXT_DIM, INNER), dtype=jnp.float32) / np.sqrt(CONTEXT_DIM)
        w_o = jax.random.normal(ks[5], (INNER, QUERY_DIM), dtype=jnp.float32) / np.sqrt(INNER)
        b_o = jax.random.normal(ks[6], (QUERY_DIM,), dtype=jnp.float32) * 0.02
        return {'x': x, 'context': context, 'w_q': w_q, 'w_k': w_k, 'w_v': w_v, 'w_o': w_o, 'b_o': b_o}
    _L0_xattn_all = _L0_xattn_setup()
    _L0_xattn_in = {k: v for k, v in _L0_xattn_all.items() if k in ('w_q', 'w_k', 'w_v', 'w_o', 'b_o')}
    del _L0_xattn_all

    def _L0_ffn_setup():
        import jax, jax.numpy as jnp
        import numpy as np
        D_MODEL = 128
        N_HEADS = 16
        D_HEAD = D_MODEL // N_HEADS
        N_EXPERTS = 8
        TOP_K = 2
        D_FF = 256
        EPS = 1e-06

        def rmsnorm(x, w):
            return x * jax.lax.rsqrt(jnp.mean(x * x, axis=-1, keepdims=True) + EPS) * w

        def swiglu(x, w_gate, w_up, w_down):
            return jax.nn.silu(x @ w_gate) * (x @ w_up) @ w_down
        key = jax.random.key(seed)
        ks = jax.random.split(key, 16)
        s = 0.02
        B, S = (2, 256)
        return {'X': jax.random.normal(ks[0], (B, S, D_MODEL), dtype=jnp.float32), 'norm1_w': jnp.ones((D_MODEL,), jnp.float32), 'norm2_w': jnp.ones((D_MODEL,), jnp.float32), 'wq': jax.random.normal(ks[1], (D_MODEL, D_MODEL), jnp.float32) * s, 'wk': jax.random.normal(ks[2], (D_MODEL, D_MODEL), jnp.float32) * s, 'wv': jax.random.normal(ks[3], (D_MODEL, D_MODEL), jnp.float32) * s, 'wo': jax.random.normal(ks[4], (D_MODEL, D_MODEL), jnp.float32) * s, 'router_w': jax.random.normal(ks[5], (D_MODEL, N_EXPERTS), jnp.float32) * s, 'sh_gate': jax.random.normal(ks[6], (D_MODEL, D_FF), jnp.float32) * s, 'sh_up': jax.random.normal(ks[7], (D_MODEL, D_FF), jnp.float32) * s, 'sh_down': jax.random.normal(ks[8], (D_FF, D_MODEL), jnp.float32) * s, 'e_gate': jax.random.normal(ks[9], (N_EXPERTS, D_MODEL, D_FF), jnp.float32) * s, 'e_up': jax.random.normal(ks[10], (N_EXPERTS, D_MODEL, D_FF), jnp.float32) * s, 'e_down': jax.random.normal(ks[11], (N_EXPERTS, D_FF, D_MODEL), jnp.float32) * s}
    _L0_ffn_all = _L0_ffn_setup()
    _L0_ffn_in = {k: v for k, v in _L0_ffn_all.items() if k in ('norm1_w', 'norm2_w', 'wq', 'wk', 'wv', 'wo', 'router_w', 'sh_gate', 'sh_up', 'sh_down', 'e_gate', 'e_up', 'e_down')}
    del _L0_ffn_all
    return {'x': x, 'ctx_768': ctx_768, 'g_xattn': g_xattn, 'g_ffn': g_ffn, 'L0_xattn_w_q': _L0_xattn_in['w_q'], 'L0_xattn_w_k': _L0_xattn_in['w_k'], 'L0_xattn_w_v': _L0_xattn_in['w_v'], 'L0_xattn_w_o': _L0_xattn_in['w_o'], 'L0_xattn_b_o': _L0_xattn_in['b_o'], 'L0_ffn_norm1_w': _L0_ffn_in['norm1_w'], 'L0_ffn_norm2_w': _L0_ffn_in['norm2_w'], 'L0_ffn_wq': _L0_ffn_in['wq'], 'L0_ffn_wk': _L0_ffn_in['wk'], 'L0_ffn_wv': _L0_ffn_in['wv'], 'L0_ffn_wo': _L0_ffn_in['wo'], 'L0_ffn_router_w': _L0_ffn_in['router_w'], 'L0_ffn_sh_gate': _L0_ffn_in['sh_gate'], 'L0_ffn_sh_up': _L0_ffn_in['sh_up'], 'L0_ffn_sh_down': _L0_ffn_in['sh_down'], 'L0_ffn_e_gate': _L0_ffn_in['e_gate'], 'L0_ffn_e_up': _L0_ffn_in['e_up'], 'L0_ffn_e_down': _L0_ffn_in['e_down']}

def reference(x, ctx_768, g_xattn, g_ffn, L0_xattn_w_q, L0_xattn_w_k, L0_xattn_w_v, L0_xattn_w_o, L0_xattn_b_o, L0_ffn_norm1_w, L0_ffn_norm2_w, L0_ffn_wq, L0_ffn_wk, L0_ffn_wv, L0_ffn_wo, L0_ffn_router_w, L0_ffn_sh_gate, L0_ffn_sh_up, L0_ffn_sh_down, L0_ffn_e_gate, L0_ffn_e_up, L0_ffn_e_down):
    import jax
    import jax.numpy as jnp

    def _L0_xattn_ref(x, context, w_q, w_k, w_v, w_o, b_o):
        import jax, jax.numpy as jnp
        import numpy as np
        HEADS = 16
        DIM_HEAD = 64
        QUERY_DIM = 128
        CONTEXT_DIM = 96
        INNER = HEADS * DIM_HEAD
        SCALE = DIM_HEAD ** (-0.5)
        B, Sq, _ = x.shape
        Skv = context.shape[1]
        q = (x @ w_q).reshape(B, Sq, HEADS, DIM_HEAD).transpose(0, 2, 1, 3)
        k = (context @ w_k).reshape(B, Skv, HEADS, DIM_HEAD).transpose(0, 2, 1, 3)
        v = (context @ w_v).reshape(B, Skv, HEADS, DIM_HEAD).transpose(0, 2, 1, 3)
        sim = jnp.einsum('bhid,bhjd->bhij', q, k) * SCALE
        attn = jax.nn.softmax(sim, axis=-1)
        out = jnp.einsum('bhij,bhjd->bhid', attn, v)
        out = out.transpose(0, 2, 1, 3).reshape(B, Sq, INNER)
        return out @ w_o + b_o

    def _L0_ffn_ref(X, norm1_w, norm2_w, wq, wk, wv, wo, router_w, sh_gate, sh_up, sh_down, e_gate, e_up, e_down):
        import jax, jax.numpy as jnp
        import numpy as np
        D_MODEL = 128
        N_HEADS = 16
        D_HEAD = D_MODEL // N_HEADS
        N_EXPERTS = 8
        TOP_K = 2
        D_FF = 256
        EPS = 1e-06

        def rmsnorm(x, w):
            return x * jax.lax.rsqrt(jnp.mean(x * x, axis=-1, keepdims=True) + EPS) * w

        def swiglu(x, w_gate, w_up, w_down):
            return jax.nn.silu(x @ w_gate) * (x @ w_up) @ w_down
        B, S, d = X.shape
        scale = 1.0 / jnp.sqrt(jnp.asarray(D_HEAD, X.dtype))
        h = rmsnorm(X, norm1_w)
        q = (h @ wq).reshape(B, S, N_HEADS, D_HEAD)
        k = (h @ wk).reshape(B, S, N_HEADS, D_HEAD)
        v = (h @ wv).reshape(B, S, N_HEADS, D_HEAD)
        scores = jnp.einsum('bshd,bthd->bhst', q, k) * scale
        attn = jax.nn.softmax(scores, axis=-1)
        ctx = jnp.einsum('bhst,bthd->bshd', attn, v).reshape(B, S, d)
        X = X + ctx @ wo
        h2 = rmsnorm(X, norm2_w).reshape(B * S, d)
        logits = h2 @ router_w
        probs = jax.nn.softmax(logits, axis=-1)
        topw, topi = jax.lax.top_k(probs, TOP_K)
        topw = jax.nn.softmax(topw, axis=-1)
        combine = jnp.sum(jax.nn.one_hot(topi, N_EXPERTS, dtype=h2.dtype) * topw[..., None], axis=1)
        shared = swiglu(h2, sh_gate, sh_up, sh_down)
        gate = jnp.einsum('td,edf->etf', h2, e_gate)
        up = jnp.einsum('td,edf->etf', h2, e_up)
        eout = jnp.einsum('etf,efd->etd', jax.nn.silu(gate) * up, e_down)
        spec = jnp.einsum('etd,te->td', eout, combine)
        moe_out = (shared + spec).reshape(B, S, d)
        return X + moe_out
    x = x + jnp.tanh(g_xattn[0]) * _L0_xattn_ref(_layernorm(x, axis=-1), ctx_768, L0_xattn_w_q, L0_xattn_w_k, L0_xattn_w_v, L0_xattn_w_o, L0_xattn_b_o)
    x = x + jnp.tanh(g_ffn[0]) * _L0_ffn_ref(_layernorm(x, axis=-1), L0_ffn_norm1_w, L0_ffn_norm2_w, L0_ffn_wq, L0_ffn_wk, L0_ffn_wv, L0_ffn_wo, L0_ffn_router_w, L0_ffn_sh_gate, L0_ffn_sh_up, L0_ffn_sh_down, L0_ffn_e_gate, L0_ffn_e_up, L0_ffn_e_down)
    return x

_drawn_inputs = setup_inputs


def setup_inputs(seed=0):
    import zlib

    import numpy as np

    out = dict(_drawn_inputs(seed))
    spreads = {'L0_ffn_norm1_w': (1.0, 0.6), 'L0_ffn_norm2_w': (1.0, 0.6)}
    factors = {'L0_xattn_b_o': 3.652, 'L0_ffn_wq': 8.0, 'L0_ffn_wk': 8.0}
    for name, (base, spread) in spreads.items():
        noise = np.random.default_rng([zlib.crc32(name.encode()), seed]).standard_normal(out[name].shape)
        drawn = base * np.exp(spread * noise) if base else spread * noise
        out[name] = jnp.asarray(drawn.astype(out[name].dtype))
    for name, factor in factors.items():
        out[name] = (out[name] * factor).astype(out[name].dtype)
    return out
```

```python
from contextlib import ExitStack
from math import log

import concourse.bass as bass
from concourse import mybir

F32 = mybir.dt.float32
F16 = mybir.dt.float16
ALU = mybir.AluOpType
ACT = mybir.ActivationFunctionType
AX = mybir.AxisListType

LN_EPS = 1e-5
RMS_EPS = 1e-6
P = 128


def flamingo_kernel(nc, x, ctx, g_xattn, g_ffn, w_q, w_k, w_v, w_o, b_o, norm1_w, norm2_w,
                    wq, wk, wv, wo, router_w, sh_gate, sh_up, sh_down, e_gate, e_up, e_down, out):
    B, S, D = x.shape
    KV, C = ctx.shape[1:]
    DH = 64
    H = w_q.shape[1] // DH
    DS = D // H
    E, _, F = e_gate.shape
    NF = F // P
    FULL = KV // P
    REM = KV - FULL * P
    CH = FULL + 1
    HALF = H // 2
    GW = 4 * S
    ROWS = H * S
    UNITS = 2 * CH
    RT = -(-ROWS // P)
    MW = 512
    MP = -(-KV // MW)
    SHIFT = 10 * log(2.0) * DH ** 0.5
    YB = [(0, 1, 2), (3, 4, 5), (6, 7)]
    YW = D + 1

    plan = {i: [] for i in range(UNITS)}
    for n, i in enumerate((3, 4, 5)):
        plan[i].append(("y1", n))
    for n, i in enumerate((15, 16, 17)):
        plan[i].append(("y0", n))
    plan[5].append(("ln", 0))
    plan[6].append(("xf", 0))
    for n, i in enumerate((7, 8, 9, 10, 11, 12, 13, 14, 15, 16, 18, 19, 20, 22)):
        plan[i].append(("f", n))
    plan[20].append(("rs", 0))
    plan[21].append(("h2", 0))
    for n, i in enumerate((2, 2, 3)):
        plan[i].append(("t", n))
    for n, i in enumerate((3, 4, 4, 5)):
        plan[i].append(("q", n))
    NPU = RT * MP
    for n in range(NPU):
        plan[6 + n * 16 // NPU].append(("p", n))
    plan[22].append(("m", 0))
    PREP = [("t", n) for n in range(3)] + [("q", n) for n in range(4)] + \
           [("p", n) for n in range(NPU)] + [("m", 0)]
    LAST = [("y1", n) for n in range(3)] + [("ln", 0), ("xf", 0)] + [("f", n) for n in range(13)] + \
           [("rs", 0), ("h2", 0), ("f", 13)]
    NO_BANK = ("ln", "xf", "rs", "h2")
    KINDS_FIRST = ("y0", "t", "q", "p", "m")
    KINDS_LAST = ("y0", "y1", "f") + NO_BANK
    flat = [u for i in range(UNITS) for u in plan[i] if u[0] not in NO_BANK]
    A = len(flat)
    A_FIRST = sum(u[0] in KINDS_FIRST for u in flat)
    A_LAST = sum(u[0] in KINDS_LAST for u in flat)
    AT_FIRST = len(PREP)
    AT_LOOP = AT_FIRST + A_FIRST

    END = AT_LOOP + A * (B - 2) + A_LAST
    TOTAL = END + sum(u[0] not in NO_BANK for u in LAST)

    def numbered(units):
        k, at = 0, {}
        for u in units:
            at[u] = k
            k += u[0] not in NO_BANK
        return at

    def steps(kind):
        kinds = {"first": KINDS_FIRST, "last": KINDS_LAST}.get(kind)
        by_place = [[u for u in plan[i] if kinds is None or u[0] in kinds] for i in range(UNITS)]
        return by_place, numbered([u for us in by_place for u in us])

    def aux_base(b, kind):
        return {"prep": 0, "first": AT_FIRST, "end": END}.get(kind, None if isinstance(b, str) else (b - 1) * A + AT_LOOP)

    ODD = {"prep": 0, "first": AT_FIRST % 2, "odd": AT_LOOP % 2, "even": (AT_LOOP + A) % 2,
           "last": (AT_LOOP + A * (B - 2)) % 2, "end": END % 2}

    def batch_of(unit, b):
        return b + {"t": 1, "q": 1, "p": 1, "m": 1, "y0": 0}.get(unit[0], -1)

    F_STEPS = ["stats", "aggr", "xf", "h", "qT", "v", "mx0", "mx1", "mx2", "mx3", "rc",
               "stats2", "aggr2", "h2"]
    NFS = len(F_STEPS)
    P_STEPS = ["var+eps", "rstd", "rstd2", "ms", "ms+eps", "r", "rr", "mean2", "ms2", "ms2+eps", "r2"]
    NPS = len(P_STEPS)
    SET_POOL = ["-1/2", "zero ident", "ident", "zero ident16", "ident16", "lnr", "Nh right", "Nh below",
                "Nh corner", "ones cT0", "pad c_hi0", "ones c_hi0", "pad c_lo0", "ones cT1", "pad c_hi1",
                "ones c_hi1", "pad c_lo1", "mx", "ones v9", "ones mask", "mask above", "head_mask",
                "n1", "wg", "wu", "rw"]
    SET_DVE = ["sum", "mean", "centred", "square", "sumsq", "lnvar", "xln", "bot", "wqT", "wkT", "wvT",
               "xlnT0", "xlnT1", "Mh0", "Mh1", "Nh0", "Nh1", "xlnT2", "xlnT3", "x1"]
    SET_PE = ["wqT", "wkT", "wvT", "xlnT0", "xlnT1", "Mh", "Nh", "xlnT2", "xlnT3"]
    Y_STEPS = 8
    EU = (E + 1) * NF

    with ExitStack() as stack:
        def sb(name, shape, dt=F32):
            return stack.enter_context(nc.sbuf_tensor(name, shape, dt))

        def sem(name):
            return stack.enter_context(nc.semaphore(name))

        ident = sb("ident", [P, P])
        ident16 = sb("ident16", [P, P], F16)
        head_mask = sb("head_mask", [P, H])
        minus_half = sb("minus_half", [P, H])
        x1 = sb("x1", [S, B, D])
        x2 = sb("x2", [S, B, D])
        xlnT = sb("xlnT", [D, B * S])
        h2T = sb("h2T", [D, B * S])
        Mh = sb("Mh", [D, H, C])
        Nh = sb("Nh", [C + 1, H, YW])
        ctx_nat = sb("ctx_nat", [P, CH, C])
        c_hi = [sb(f"c_hi{q}", [P, CH, P], F16) for q in range(2)]
        c_lo = [sb(f"c_lo{q}", [P, CH, P], F16) for q in range(2)]
        cT_hi = [sb(f"cT_hi{q}", [C + 1, KV], F16) for q in range(2)]
        cT_lo = [sb(f"cT_lo{q}", [C, KV], F16) for q in range(2)]
        qk_hi = [sb(f"qk_hi{q}", [C + 1, ROWS], F16) for q in range(2)]
        qk_lo = [sb(f"qk_lo{q}", [C, ROWS], F16) for q in range(2)]
        p32 = sb("p32", [P, 3, 2, GW])
        p_hi = sb("p_hi", [P, 3, 2, GW], F16)
        p_lo = sb("p_lo", [P, 3, 2, GW], F16)
        acc_sb = [sb(f"acc_sb{g}", [C + 1, 2, GW]) for g in range(2)]
        mx = sb("mx", [P, RT, MP])
        mx_row = sb("mx_row", [P, RT])
        mneg = sb("mneg", [P, RT], F16)
        mrow = sb("mrow", [RT, P], F16)
        y_rc = sb("y_rc", [S, 3])
        n1 = sb("n1", [D, 1])
        n2 = sb("n2", [D, 1])
        sw = sb("sw", [D, 4, D])
        stats = sb("stats", [S, 6])
        aggr = sb("aggr", [S, 2])
        stats2 = sb("stats2", [S, 6])
        aggr2 = sb("aggr2", [S, 2])
        ps = sb("ps", [S, NPS])
        xf = sb("xf", [S, D])
        hn = sb("hn", [S, D])
        hT = sb("hT", [D, S])
        qT = sb("qT", [D, S])
        kbd = sb("kbd", [D, H, S])
        v9 = sb("v9", [S, H, DS + 1])
        mx4 = sb("mx4", [S, 4, 4])
        ex = sb("ex", [S, 4, 4, S])
        pT = sb("pT", [S, 4, GW])
        s_rc = sb("s_rc", [S, H])
        sctx = sb("sctx", [S, H, DS])
        sctxT = sb("sctxT", [D, S])
        hn2 = sb("hn2", [S, D])
        wg = sb("wg", [D, E + 1, F])
        wu = sb("wu", [D, E + 1, F])
        wd = sb("wd", [P, E + 1, NF, D])
        rw = sb("rw", [D, E])
        gx = sb("gx", [P, 1])
        gf = sb("gf", [P, 1])
        tx = sb("tx", [P, 1])
        tf = sb("tf", [P, 1])
        bo = sb("bo", [S, D])

        psum = stack.enter_context(nc.psum_tensor("psum", [P, 8, 512], F32))
        ACCB, AUXB = 4, 6

        names = ["w_in", "e_in", "set_pool", "set_dve", "set_act", "set_pe",
                 "ctx_in", "row_in", "split", "scores", "probs_hi", "probs_lo", "pv", "acc_out",
                 "aux_full", "aux_free", "hi_out", "max_step", "y_step", "f_step", "pool_step",
                 "exp_out", "logit_full", "top", "gu_full", "silu_out", "hid", "down_full", "sum2",
                 "fin", "out_done"]
        sm = {n: sem(n) for n in names}
        w_in, e_in, set_pool, set_dve, set_act, set_pe = (sm[n] for n in names[:6])
        ctx_in, row_in, split, scores, probs_hi, probs_lo, pv, acc_out = (sm[n] for n in names[6:14])
        aux_full, aux_free, hi_out, max_step, y_step, f_step, pool_step = (sm[n] for n in names[14:21])
        exp_out, logit_full, top, gu_full, silu_out, hid, down_full, sum2, fin, out_done = \
            (sm[n] for n in names[21:])

        def f_at(c, name):
            return c * NFS + (F_STEPS.index(name) + 1)

        def p_at(c, name):
            return c * NPS + (P_STEPS.index(name) + 1)

        def pcol(name):
            k = P_STEPS.index(name)
            return ps[:, k:k + 1]

        def set_wait(eng, signal, order, name):
            eng.wait_ge(signal, order.index(name) + 1)

        def wait_apart(eng, signal, value):
            if not isinstance(value, int):
                value = eng.to_reg(value)
                eng.wait_ge(w_in, 16)
            eng.wait_ge(signal, value)

        def batches(eng, body):
            body(0, "first", 0)
            with eng.Fori(0, (B - 2) // 2) as r:
                body(r * 2 + 1, "odd", 1)
                body(r * 2 + 2, "even", 0)
            body(B - 1, "last", 1)

        def groups(eng, body):
            body(0)
            with eng.Fori(1, B // 4) as q:
                body(q)

        def wait_past(eng, signal, value):
            if not (isinstance(value, int) and value == 0):
                eng.wait_ge(signal, value)

        def run_aux(aux, units, b, kind, parity):
            at = {"prep": numbered(PREP), "end": numbered(LAST)}.get(kind) or steps(kind)[1]
            base = aux_base(b, kind)
            for u in units:
                on = 0 if kind == "prep" else batch_of(u, b)
                near = 0 if kind == "prep" else batch_of(u, 0)
                aux(base + at[u], (ODD[kind] + at[u]) % 2, u, on, (parity + near) % 2,
                    lambda other: base + at[other])

        def cut(q, n):
            return slice(q * n, q * n + n) if isinstance(q, int) else bass.ds(q * n, n)

        def tok(b):
            return slice(b * S, b * S + S) if isinstance(b, int) else bass.ds(b * S, S)

        def bat(b, n=1):
            return slice(b, b + n) if isinstance(b, int) else bass.ds(b, n)

        def kc(j):
            m = P if j < FULL else REM
            return slice(j * P, j * P + m), m

        def rows_of(t):
            return min(P, ROWS - t * P)

        NSPLIT = 4
        W_LOADS, E_LOADS = 13, 2 * 2 + E + 1 + 2
        T_SUB, T_D = 2, 2 + 3 + E + 11 + 1

        wq_nat = p32[:, :, :, :].rearrange("p a k w -> p (a k w)")[:, 0:H * DH]
        wk_nat = sb("wk_nat", [C, H * DH])
        wv_nat = sb("wv_nat", [C, H * DH])
        wo_nat = sb("wo_nat", [P, H // 2, D])
        wqT = sb("wqT", [P, H // 2, D])
        wkT = sb("wkT", [P, H // 2, C])
        wvT = sb("wvT", [P, H // 2, C])
        xc = x2
        lnsum = sb("lnsum", [S, B])
        lnvar = sb("lnvar", [S, B])
        lnr = sb("lnr", [S, B])
        bot = sb("bot", [S, D])
        sqb = sb("sqb", [S, B, D])
        rt_m = sb("rt_m", [S, B])
        rt_a = sb("rt_a", [S, B])
        rt_b = sb("rt_b", [S, B])
        rt_e = sb("rt_e", [S, B])
        rt_p = sb("rt_p", [S, B, E])
        rt_no = sb("rt_no", [S, B, E])
        rt_s = [sb(f"rt_s{k}", [S, B, E]) for k in range(2)]
        comb = sb("comb", [S, B, E + 1])
        silu = p32[:, :, 0, :]
        hidden = p32[:, :, 1, :]

        block = stack.enter_context(nc.Block())

        @block.sync
        def _(sp):
            def load(dst, src, signal=w_in):
                sp.dma_start(dst, src).then_inc(signal, 16)

            def load_ctx(b):
                sp.dma_start(ctx_nat[:, 0:FULL, :], ctx[bat(b), 0:FULL * P, :].rearrange(
                    "b (p j) c -> p (b j) c", j=FULL)).then_inc(ctx_in, 16)
                sp.dma_start(ctx_nat[0:REM, FULL, :], ctx[bat(b), FULL * P:KV, :].rearrange(
                    "b r c -> (b r) c")).then_inc(ctx_in, 16)

            def send_row(b, parity, seq):
                sp.wait_ge(aux_free, seq + 1)
                sp.dma_start(qk_hi[parity][C:C + 1, 0:(RT - 1) * P], mrow[0:RT - 1, :]).then_inc(row_in, 16)
                sp.dma_start(qk_hi[parity][C:C + 1, (RT - 1) * P:ROWS],
                             mrow[RT - 1:RT, 0:rows_of(RT - 1)]).then_inc(row_in, 16)

            load(x1[:, :, :], x.rearrange("b s d -> s b d"))
            load_ctx(0)
            load(wq_nat, w_q)
            load(wk_nat[:, :], w_k)
            load(wv_nat[:, :], w_v)
            load(wo_nat[:, :, :], w_o.rearrange("(a k) d -> k a d", k=P))
            load(gx[:, :], g_xattn.partition_broadcast(P))
            load(gf[:, :], g_ffn.partition_broadcast(P))
            load(bo[:, :], b_o.partition_broadcast(S))
            load(n1[:, :], norm1_w.rearrange("(p a) -> p a", a=1))
            for k, w in enumerate((wq, wk, wv, wo)):
                load(sw[:, k, :], w)
            load(n2[:, :], norm2_w.rearrange("(p a) -> p a", a=1), e_in)
            load(rw[:, :], router_w, e_in)
            for dst, many, one in ((wg, e_gate, sh_gate), (wu, e_up, sh_up)):
                load(dst[:, 0:E, :], many.rearrange("e d f -> d e f"), e_in)
                load(dst[:, E, :], one, e_in)
            for e in range(E):
                load(wd[:, e, :, :], e_down[e].rearrange("(a p) d -> p a d", p=P), e_in)
            load(wd[:, E, :, :], sh_down.rearrange("(a p) d -> p a d", p=P), e_in)
            send_row(0, 0, len(PREP) - 1)

            def body(b, kind, parity):
                if kind == "last":
                    return
                sp.wait_ge(hi_out, b * 7 + 3)
                sp.wait_ge(split, (b + 1) * NSPLIT)
                load_ctx(b + 1)
                if kind != "first":
                    sp.wait_ge(scores, b * UNITS)
                send_row(b + 1, 1 - parity, aux_base(b, kind) + steps(kind)[1][("m", 0)])

            batches(sp, body)
            for q in range(4):
                sp.wait_ge(fin, q + 1)
                sp.dma_start(out[4 * q:4 * q + 4].rearrange("b s d -> s b d"),
                             sqb[:, 4 * q:4 * q + 4, :]).then_inc(out_done, 16)
            sp.wait_ge(out_done, 64)

        @block.gpsimd
        def _(pool):
            g = nc.gpsimd

            def step(name, ins):
                ins.then_inc(set_pool, 1)
                set_wait(pool, set_pool, SET_POOL, name)

            def select(t, base, pattern, cm, op, fill):
                return g.affine_select(out=t[:, :], in_=t[:, :], compare_op=op, fill=fill, base=base,
                                       pattern=pattern, channel_multiplier=cm)

            step("-1/2", g.memset(minus_half[:, :], -0.5))
            step("zero ident", g.memset(ident[:, :], 0.0))
            step("ident", select(ident, 0, [[-1, P]], 1, ALU.not_equal, 1.0))
            step("zero ident16", g.memset(ident16[:, :], 0.0))
            step("ident16", select(ident16, 0, [[-1, P]], 1, ALU.not_equal, 1.0))
            set_wait(pool, set_dve, SET_DVE, "lnvar")
            step("lnr", g.tensor_tensor(lnr[:, :], lnvar[:, :], minus_half[0:S, :], ALU.pow))
            step("Nh right", g.memset(Nh[:, :, D:YW], 0.0))
            step("Nh below", g.memset(Nh[C:C + 1, :, 0:D], 0.0))
            step("Nh corner", g.memset(Nh[C:C + 1, :, D:YW], 1.0))
            for q in range(2):
                step(f"ones cT{q}", g.memset(cT_hi[q][C:C + 1, :], 1.0))
                step(f"pad c_hi{q}", g.memset(c_hi[q][:, :, C:P], 0.0))
                step(f"ones c_hi{q}", g.memset(c_hi[q][:, :, C:C + 1], 1.0))
                step(f"pad c_lo{q}", g.memset(c_lo[q][:, :, C:P], 0.0))
            step("mx", g.memset(mx[:, :, :], 0.0))
            step("ones v9", g.memset(v9[:, :, DS:DS + 1], 1.0))
            step("ones mask", g.memset(head_mask[:, :], 1.0))
            step("mask above", select(head_mask, 0, [[-DS, H]], 1, ALU.is_ge, 0.0))
            step("head_mask", select(head_mask, DS - 1, [[DS, H]], -1, ALU.is_ge, 0.0))

            def split_ctx(b, kind, parity):
                wait_apart(pool, ctx_in, (b + 1) * 32)
                if kind not in ("prep", "first"):
                    wait_apart(pool, pv, (b - 1) * UNITS)
                for n, (r, js) in enumerate(((P, slice(0, FULL)), (REM, slice(FULL, CH)))):
                    g.tensor_copy(c_hi[parity][0:r, js, 0:C], ctx_nat[0:r, js, :]).then_inc(split, 1)
                    pool.wait_ge(split, b * NSPLIT + (2 * n + 1))
                    g.tensor_tensor(c_lo[parity][0:r, js, 0:C], ctx_nat[0:r, js, :],
                                    c_hi[parity][0:r, js, 0:C], ALU.subtract).then_inc(split, 1)

            def small(c, name, ins):
                ins.then_inc(pool_step, 1)
                wait_apart(pool, pool_step, p_at(c, name))

            def norms(c):
                half = minus_half[0:S, 0:1]
                var = aggr[:, 1:2]
                wait_apart(pool, f_step, f_at(c, "aggr"))
                small(c, "var+eps", g.tensor_scalar(pcol("var+eps"), var, LN_EPS, None, ALU.add))
                small(c, "rstd", g.tensor_tensor(pcol("rstd"), pcol("var+eps"), half, ALU.pow))
                small(c, "rstd2", g.tensor_tensor(pcol("rstd2"), pcol("rstd"), pcol("rstd"), ALU.mult))
                small(c, "ms", g.tensor_tensor(pcol("ms"), pcol("rstd2"), var, ALU.mult))
                small(c, "ms+eps", g.tensor_scalar(pcol("ms+eps"), pcol("ms"), RMS_EPS, None, ALU.add))
                small(c, "r", g.tensor_tensor(pcol("r"), pcol("ms+eps"), half, ALU.pow))
                small(c, "rr", g.tensor_tensor(pcol("rr"), pcol("r"), pcol("rstd"), ALU.mult))
                pool.wait_ge(f_step, f_at(c, "aggr2"))
                small(c, "mean2", g.tensor_tensor(pcol("mean2"), aggr2[:, 0:1], aggr2[:, 0:1], ALU.mult))
                small(c, "ms2", g.tensor_tensor(pcol("ms2"), pcol("mean2"), aggr2[:, 1:2], ALU.add))
                small(c, "ms2+eps", g.tensor_scalar(pcol("ms2+eps"), pcol("ms2"), RMS_EPS, None, ALU.add))
                small(c, "r2", g.tensor_tensor(pcol("r2"), pcol("ms2+eps"), half, ALU.pow))

            split_ctx(0, "prep", 0)
            step("n1", g.tensor_scalar(sw[:, 0:3, :], sw[:, 0:3, :], n1[:, 0:1], None, ALU.mult))
            pool.wait_ge(e_in, 16 * E_LOADS)
            for name, w in (("wg", wg[:, :, :]), ("wu", wu[:, :, :]), ("rw", rw[:, :])):
                step(name, g.tensor_scalar(w, w, n2[:, 0:1], None, ALU.mult))

            def body(b, kind, parity):
                if kind != "last":
                    split_ctx(b + 1, kind, 1 - parity)
                if kind != "first":
                    norms(b - 1)

            batches(pool, body)
            norms(B - 1)

        @block.tensor
        def _(pe):
            mm = nc.tensor.matmul
            tr = nc.tensor.transpose

            pe.wait_ge(w_in, 16 * W_LOADS)
            set_wait(pe, set_pool, SET_POOL, "lnr")
            for a in range(H // 2):
                t = tr(psum[:, a // 4, (a % 4) * D:(a % 4) * D + D], wq_nat[:, a * P:(a + 1) * P], ident[:, :])
            t.then_inc(set_pe, 1)
            for k, w in enumerate((wk_nat, wv_nat)):
                for a in range(H // 2):
                    t = tr(psum[:, 2 + 2 * k + a // 4, (a % 4) * C:(a % 4) * C + C],
                           w[:, a * P:(a + 1) * P], ident[0:C, 0:C])
                t.then_inc(set_pe, 1)
            set_wait(pe, set_dve, SET_DVE, "xln")
            for g in range(2):
                for k in range(4):
                    t = tr(psum[:, AUXB + g, k * S:(k + 1) * S], xc[:, 4 * g + k, :], ident[0:S, 0:S])
                t.then_inc(set_pe, 1)
            set_wait(pe, set_dve, SET_DVE, "wkT")
            for r in range(2):
                for a in range(H // 2):
                    rs = slice(DH * r, DH * r + DH)
                    t = mm(psum[:, 2 * r + a // 4, (a % 4) * C:(a % 4) * C + C], wqT[rs, a, :], wkT[rs, a, :],
                           start=True, stop=True)
            t.then_inc(set_pe, 1)
            set_wait(pe, set_dve, SET_DVE, "xlnT1")
            for r in range(2):
                for a in range(H // 2):
                    rs = slice(DH * r, DH * r + DH)
                    t = mm(psum[0:C, 4 + 2 * r + a // 4, (a % 4) * D:(a % 4) * D + D], wvT[rs, a, :],
                           wo_nat[rs, a, :], start=True, stop=True)
            t.then_inc(set_pe, 1)
            set_wait(pe, set_dve, SET_DVE, "Mh1")
            for g in range(2, 4):
                for k in range(4):
                    t = tr(psum[:, g - 2, k * S:(k + 1) * S], xc[:, 4 * g + k, :], ident[0:S, 0:S])
                t.then_inc(set_pe, 1)
            set_wait(pe, set_dve, SET_DVE, "xlnT3")

            set_wait(pe, set_pool, SET_POOL, "head_mask")

            def score_unit(b, parity, i):
                g, j = divmod(i, CH)
                cols, m = kc(j)
                if isinstance(b, int) and b == 0 and i < 2:
                    pass
                else:
                    pe.wait_ge(probs_hi, b * UNITS + (i - 1))
                if i == 0:
                    pe.wait_ge(row_in, (b + 1) * 32)
                s = i % 2
                outs = [psum[0:m, 2 * s + k, 0:GW] for k in range(2)]
                qs = [slice((2 * g + k) * GW, (2 * g + k + 1) * GW) for k in range(2)]
                for k in range(2):
                    mm(outs[k], cT_hi[parity][:, cols], qk_hi[parity][:, qs[k]], start=True, stop=False)
                for k in range(2):
                    mm(outs[k], cT_hi[parity][0:C, cols], qk_lo[parity][:, qs[k]], start=False, stop=False)
                for k in range(2):
                    t = mm(outs[k], cT_lo[parity][:, cols], qk_hi[parity][0:C, qs[k]], start=False, stop=True)
                t.then_inc(scores, 1)

            def pv_unit(b, parity, i):
                j = i % CH
                m = kc(j)[1]
                pe.wait_ge(probs_lo, b * UNITS + (i + 1))
                if i == 0:
                    pe.wait_ge(split, (b + 1) * NSPLIT)
                if j == 0 and not (isinstance(b, int) and b == 0 and i == 0):
                    pe.wait_ge(acc_out, b * 2 + i // CH)
                outs = [psum[:, ACCB + k, 0:GW] for k in range(2)]
                for w, p in ((c_hi, p_hi), (c_hi, p_lo), (c_lo, p_hi)):
                    for k in range(2):
                        t = mm(outs[k], w[parity][0:m, j, :], p[0:m, i % 3, k, :],
                               start=(j == 0 and w is c_hi and p is p_hi), stop=(j == CH - 1 and w is c_lo))
                t.then_inc(pv, 1)

            def aux(seq, par, unit, b, parity, before):
                kind, n = unit
                if kind in NO_BANK:
                    return
                if not (isinstance(seq, int) and seq < 2):
                    pe.wait_ge(aux_free, seq - 1)
                bank = psum[:, AUXB + par, :]
                if kind == "t":
                    if n == 0:
                        pe.wait_ge(ctx_in, (b + 1) * 32)
                    for k in range(4):
                        m = kc(4 * n + k)[1]
                        t = tr(bank[0:C, k * P:k * P + m], ctx_nat[0:m, 4 * n + k, :], ident[0:m, 0:m])
                elif kind == "q":
                    for k in range(4):
                        t = mm(bank[0:C, k * S:(k + 1) * S], Mh[:, 4 * n + k, :], xlnT[:, tok(b)],
                               start=True, stop=True)
                elif kind == "p":
                    rt, part = divmod(n, MP)
                    if n == 0:
                        pe.wait_ge(aux_free, seq)
                    r = rows_of(rt)
                    w = min(MW, KV - part * MW)
                    t = mm(bank[0:r, 0:w], qk_hi[parity][0:C, rt * P:rt * P + r],
                           cT_hi[parity][0:C, part * MW:part * MW + w], start=True, stop=True)
                elif kind == "m":
                    pe.wait_ge(max_step, (b + 1) * 2)
                    t = tr(bank[0:RT, 0:P // 2].bitcast(F16), mneg[:, :], ident16[:, :])
                elif kind in ("y0", "y1"):
                    half = int(kind[1])
                    if n == 0:
                        pe.wait_ge(acc_out, b * 2 + (half + 1))
                    for k, h in enumerate(YB[n]):
                        t = mm(bank[0:S, k * YW:(k + 1) * YW], acc_sb[half][:, h // 4, (h % 4) * S:(h % 4 + 1) * S],
                               Nh[:, half * HALF + h, :], start=True, stop=True)
                elif n == 0:
                    pe.wait_ge(f_step, f_at(b, "h"))
                    t = tr(bank[:, 0:S], hn[:, :], ident[0:S, 0:S])
                elif n == 1:
                    pe.wait_ge(aux_free, before(("f", 0)) + 1)
                    mm(bank[:, 0:S], sw[:, 0, :], hT[:, :], start=True, stop=True)
                    mm(bank[:, P:P + S], sw[:, 1, :], hT[:, :], start=True, stop=True)
                    t = mm(bank[0:S, 2 * P:3 * P], hT[:, :], sw[:, 2, :], start=True, stop=True)
                elif n < 6:
                    if n == 2:
                        pe.wait_ge(aux_free, before(("f", 1)) + 1)
                    t = mm(bank[0:S, 0:GW], qT[:, :], kbd[:, 4 * (n - 2):4 * (n - 1), :].rearrange("p a s -> p (a s)"),
                           start=True, stop=True)
                elif n < 10:
                    pe.wait_ge(exp_out, b * 4 + (n - 5))
                    for k in range(4):
                        t = tr(bank[0:S, k * S:(k + 1) * S], ex[:, n - 6, k, :], ident[0:S, 0:S])
                elif n == 10:
                    pe.wait_ge(aux_free, before(("f", 9)) + 1)
                    for h in range(H):
                        t = mm(bank[0:S, h * (DS + 1):(h + 1) * (DS + 1)], pT[:, h // 4, (h % 4) * S:(h % 4 + 1) * S],
                               v9[:, h, :], start=True, stop=True)
                elif n == 11:
                    pe.wait_ge(aux_free, before(("f", 10)) + 1)
                    t = tr(bank[:, 0:S], sctx[:, :, :].rearrange("p h d -> p (h d)"), ident[0:S, 0:S])
                elif n == 12:
                    pe.wait_ge(aux_free, before(("f", 11)) + 1)
                    t = mm(bank[0:S, 0:D], sctxT[:, :], sw[:, 3, :], start=True, stop=True)
                else:
                    pe.wait_ge(f_step, f_at(b, "h2"))
                    t = tr(bank[:, 0:S], hn2[:, :], ident[0:S, 0:S])
                t.then_inc(aux_full, 1)

            run_aux(aux, PREP, 0, "prep", 0)

            def body(b, kind, parity):
                for i in range(UNITS):
                    score_unit(b, parity, i)
                    run_aux(aux, steps(kind)[0][i], b, kind, parity)
                    if i >= 2:
                        pv_unit(b, parity, i - 2)
                    elif kind != "first":
                        pv_unit(b - 1, 1 - parity, UNITS - 2 + i)

            batches(pe, body)
            for i in (UNITS - 2, UNITS - 1):
                pv_unit(B - 1, 1, i)
            run_aux(aux, LAST, B, "end", 0)

            pe.wait_ge(aux_free, TOTAL)
            set_wait(pe, set_pool, SET_POOL, "rw")
            for b in range(B):
                t = mm(psum[0:S, ACCB + 1, b * E:(b + 1) * E], h2T[:, tok(b)], rw[:, :], start=True, stop=True)
            t.then_inc(logit_full, 1)

            def gate_up(q, n):
                e, f = divmod(n, NF)
                wait_past(pe, hid, q * EU + max(n - 1, 0))
                for k, w in enumerate((wg, wu)):
                    t = mm(psum[:, 2 * (n % 2) + k, 0:GW], w[:, e, f * P:(f + 1) * P], h2T[:, cut(q, GW)],
                           start=True, stop=True)
                t.then_inc(gu_full, 1)

            def down(q, n):
                e, f = divmod(n, NF)
                pe.wait_ge(hid, q * EU + (n + 1))
                if f == 0 and e >= 2:
                    pe.wait_ge(sum2, q * 4 * (E + 1) + 4 * (e - 1))
                elif f == 0:
                    wait_past(pe, sum2, q * 4 * (E + 1))
                for k in range(4):
                    t = mm(psum[0:S, AUXB + e % 2, k * D:(k + 1) * D], hidden[:, n % 3, k * S:(k + 1) * S],
                           wd[:, e, f, :], start=(f == 0 and k == 0), stop=(f == NF - 1 and k == 3),
                           skip_group_check=True)
                t.then_inc(down_full, 1)

            def group(q):
                for n in range(EU + 2):
                    if n < EU:
                        gate_up(q, n)
                    if n >= 2:
                        down(q, n - 2)

            groups(pe, group)

        @block.scalar
        def _(act):
            a = nc.scalar.activation
            act.wait_ge(w_in, 16 * W_LOADS)
            a(tx[:, :], gx[:, :], ACT.Tanh).then_inc(set_act, 1)
            a(tf[:, :], gf[:, :], ACT.Tanh).then_inc(set_act, 1)

            def evac_hi(seq, par, unit, parity):
                kind, n = unit
                act.wait_ge(aux_full, seq + 1)
                if kind == "t":
                    w = min(512, KV - 512 * n)
                    a(cT_hi[parity][0:C, 512 * n:512 * n + w], psum[0:C, AUXB + par, 0:w], ACT.Copy).then_inc(hi_out, 1)
                else:
                    a(qk_hi[parity][0:C, GW * n:GW * (n + 1)], psum[0:C, AUXB + par, 0:GW], ACT.Copy).then_inc(hi_out, 1)

            def probs(b, i):
                m = kc(i % CH)[1]
                act.wait_ge(scores, b * UNITS + (i + 1))
                if not (isinstance(b, int) and b == 0 and i < 3):
                    act.wait_ge(probs_lo, b * UNITS + (i - 2))
                    act.wait_ge(pv, b * UNITS + (i - 2))
                src = psum[0:m, 2 * (i % 2):2 * (i % 2) + 2, 0:GW]
                a(p32[0:m, i % 3, :, :], src, ACT.Exp, scale=DH ** -0.5)
                a(p_hi[0:m, i % 3, :, :], src, ACT.Exp, scale=DH ** -0.5).then_inc(probs_hi, 1)

            def acc_evac(b, half):
                act.wait_ge(pv, b * UNITS + (half + 1) * CH)
                a(acc_sb[half][:, :, :], psum[0:C + 1, ACCB:ACCB + 2, 0:GW], ACT.Copy).then_inc(acc_out, 1)

            def self_exp(seq, c, g):
                act.wait_ge(aux_free, seq + 1)
                a(ex[:, g, :, :], ex[:, g, :, :], ACT.Exp, scale=DS ** -0.5).then_inc(exp_out, 1)

            def aux(seq, par, unit, b, parity, before):
                if unit[0] in ("t", "q"):
                    evac_hi(seq, par, unit, parity)
                elif unit[0] == "f" and 2 <= unit[1] < 6:
                    self_exp(seq, b, unit[1] - 2)

            run_aux(aux, PREP, 0, "prep", 0)

            def body(b, kind, parity):
                for i in range(UNITS):
                    probs(b, i)
                    if i == 2 and kind not in ("first", "last"):
                        act.wait_ge(scores, b * UNITS)
                    run_aux(aux, steps(kind)[0][i], b, kind, parity)
                    if i == 1 and kind != "first":
                        acc_evac(b - 1, 1)
                    if i == CH + 1:
                        acc_evac(b, 0)

            batches(act, body)
            acc_evac(B - 1, 1)
            run_aux(aux, LAST, B, "end", 0)

            act.wait_ge(top, T_SUB)
            a(rt_p[:, :, :], rt_p[:, :, :], ACT.Exp).then_inc(silu_out, 1)
            act.wait_ge(top, T_D)
            a(rt_e[:, :], rt_e[:, :], ACT.Exp).then_inc(silu_out, 1)
            def group(q):
                for n in range(EU):
                    act.wait_ge(gu_full, q * EU + (n + 1))
                    wait_past(act, hid, q * EU + max(n - 2, 0))
                    a(silu[:, n % 3, :], psum[:, 2 * (n % 2), 0:GW], ACT.Silu).then_inc(silu_out, 1)

            groups(act, group)

        @block.vector
        def _(dve):
            v = nc.vector
            tt, ts, stt, cp = v.tensor_tensor, v.tensor_scalar, v.scalar_tensor_tensor, v.tensor_copy

            def step(name, ins, wait=True):
                ins.then_inc(set_dve, 1)
                if wait:
                    set_wait(dve, set_dve, SET_DVE, name)

            def per_token(t):
                return t.unsqueeze(2).broadcast_to([S, B, D])

            dve.wait_ge(w_in, 16 * W_LOADS)
            step("sum", v.tensor_reduce(lnsum[:, :], x1[:, :, :], AX.X, ALU.add))
            step("mean", ts(lnsum[:, :], lnsum[:, :], 1.0 / D, None, ALU.mult))
            step("centred", tt(xc[:, :, :], x1[:, :, :], per_token(lnsum[:, :]), ALU.subtract))
            step("square", tt(sqb[:, :, :], xc[:, :, :], xc[:, :, :], ALU.mult))
            step("sumsq", v.tensor_reduce(lnvar[:, :], sqb[:, :, :], AX.X, ALU.add))
            step("lnvar", ts(lnvar[:, :], lnvar[:, :], 1.0 / D, LN_EPS, ALU.mult, ALU.add))
            set_wait(dve, set_pool, SET_POOL, "lnr")
            step("xln", tt(xc[:, :, :], xc[:, :, :], per_token(lnr[:, :]), ALU.mult))
            dve.wait_ge(set_act, 1)
            step("bot", ts(bot[:, :], bo[:, :], tx[0:S, 0:1], None, ALU.mult))
            set_wait(dve, set_pe, SET_PE, "wqT")
            step("wqT", cp(wqT[:, :, :].rearrange("p (a k) d -> p a (k d)", a=2), psum[:, 0:2, :]))
            set_wait(dve, set_pe, SET_PE, "wkT")
            step("wkT", cp(wkT[:, :, :].rearrange("p (a k) c -> p a (k c)", a=2), psum[:, 2:4, 0:4 * C]))
            set_wait(dve, set_pe, SET_PE, "wvT")
            step("wvT", cp(wvT[:, :, :].rearrange("p (a k) c -> p a (k c)", a=2), psum[:, 4:6, 0:4 * C]))
            for g in range(2):
                set_wait(dve, set_pe, SET_PE, f"xlnT{g}")
                step(f"xlnT{g}", cp(xlnT[:, g * GW:(g + 1) * GW], psum[:, AUXB + g, 0:GW]))
            Mh_r = Mh[:, :, :].rearrange("p (a r) c -> p r a c", r=2)
            Nh_r = Nh[0:C, :, :].rearrange("p (a r) c -> p r a c", r=2)
            set_wait(dve, set_pe, SET_PE, "Mh")
            for r in range(2):
                cp(Mh_r[:, r, 0:4, :], psum[:, 2 * r, 0:4 * C].rearrange("p (k c) -> p k c", c=C))
                step(f"Mh{r}", cp(Mh_r[:, r, 4:8, :],
                                  psum[:, 2 * r + 1, 0:4 * C].rearrange("p (k c) -> p k c", c=C)))
            set_wait(dve, set_pe, SET_PE, "Nh")
            for r in range(2):
                for h in range(2):
                    ins = ts(Nh_r[:, r, 4 * h:4 * h + 4, 0:D],
                             psum[0:C, 4 + 2 * r + h, :].rearrange("p (k c) -> p k c", c=D),
                             tx[0:C, 0:1], None, ALU.mult)
                step(f"Nh{r}", ins)
            for g in range(2, 4):
                set_wait(dve, set_pe, SET_PE, f"xlnT{g}")
                step(f"xlnT{g}", cp(xlnT[:, g * GW:(g + 1) * GW], psum[:, g - 2, 0:GW]))
            step("x1", tt(x1[:, :, :], x1[:, :, :], bot[:, :].unsqueeze(1).broadcast_to([S, B, D]), ALU.add))

            set_wait(dve, set_pool, SET_POOL, "head_mask")

            def probs_rest(b, i):
                m = kc(i % CH)[1]
                dve.wait_ge(probs_hi, b * UNITS + (i + 1))
                if not (isinstance(b, int) and b == 0 and i < 3):
                    dve.wait_ge(pv, b * UNITS + (i - 2))
                tt(p_lo[0:m, i % 3, :, :], p32[0:m, i % 3, :, :], p_hi[0:m, i % 3, :, :],
                   ALU.subtract).then_inc(probs_lo, 1)

            def f_inc(ins, c, name, wait=False):
                ins.then_inc(f_step, 1)
                if wait:
                    wait_apart(dve, f_step, f_at(c, name))

            def aux(seq, par, unit, b, parity, before):
                kind, n = unit
                bank = psum[:, AUXB + par, :]
                if kind == "ln":
                    wait_apart(dve, aux_free, seq)
                    f_inc(v.bn_stats(stats[:, :], x1[:, bat(b), :]), b, "stats", True)
                    f_inc(v.bn_aggr(aggr[:, :], stats[:, :]), b, "aggr", True)
                    return
                if kind == "xf":
                    dve.wait_ge(pool_step, p_at(b, "rr"))
                    f_inc(ts(xf[:, :], x1[:, bat(b), :].squeeze(1), aggr[:, 0:1], pcol("rstd"),
                             ALU.subtract, ALU.mult), b, "xf")
                    f_inc(ts(hn[:, :], x1[:, bat(b), :].squeeze(1), aggr[:, 0:1], pcol("rr"),
                             ALU.subtract, ALU.mult), b, "h", True)
                    return
                if kind == "rs":
                    wait_apart(dve, aux_free, seq)
                    f_inc(v.bn_stats(stats2[:, :], x2[:, bat(b), :]), b, "stats2", True)
                    f_inc(v.bn_aggr(aggr2[:, :], stats2[:, :]), b, "aggr2", True)
                    return
                if kind == "h2":
                    dve.wait_ge(pool_step, p_at(b, "r2"))
                    f_inc(ts(hn2[:, :], x2[:, bat(b), :].squeeze(1), pcol("r2"), None, ALU.mult), b, "h2")
                    return
                if kind in ("t", "q"):
                    dve.wait_ge(hi_out, b * 7 + (n + 1 + 3 * (kind == "q")))
                    if kind == "t":
                        cols = slice(512 * n, min(KV, 512 * (n + 1)))
                        hi, lo = cT_hi[parity][0:C, cols], cT_lo[parity][:, cols]
                        w = cols.stop - cols.start
                    else:
                        w = GW
                        hi, lo = (t[parity][0:C, GW * n:GW * (n + 1)] for t in (qk_hi, qk_lo))
                    tt(lo, bank[0:C, 0:w], hi, ALU.subtract).then_inc(aux_free, 1)
                    return
                dve.wait_ge(aux_full, seq + 1)
                if kind == "p":
                    rt, part = divmod(n, MP)
                    w = min(MW, KV - part * MW)
                    r = rows_of(rt)
                    v.tensor_reduce(mx[0:r, rt, part:part + 1], bank[0:r, 0:w], AX.X, ALU.max)\
                        .then_inc(aux_free, 1)
                    if n == NPU - 1:
                        dve.wait_ge(aux_free, seq + 1)
                        v.tensor_reduce(mx_row[:, :], mx[:, :, :], AX.X, ALU.max).then_inc(max_step, 1)
                        dve.wait_ge(max_step, b * 2 + 1)
                        ts(mneg[:, :], mx_row[:, :], -1.0, SHIFT, ALU.mult, ALU.add).then_inc(max_step, 1)
                elif kind == "m":
                    if not (isinstance(b, int) and b == 0):
                        dve.wait_ge(row_in, b * 32)
                    cp(mrow[:, :], bank[0:RT, 0:P // 2].bitcast(F16)).then_inc(aux_free, 1)
                elif kind in ("y0", "y1"):
                    half = int(kind[1])
                    at = half * Y_STEPS + sum(len(YB[k]) for k in range(n)) + 1
                    nh = len(YB[n])
                    heads = bank[0:S, 0:nh * YW].rearrange("p (k w) -> p k w", w=YW)
                    xb = x1[:, bat(b), :].squeeze(1)
                    dve.wait_ge(aux_free, seq)
                    v.reciprocal(y_rc[:, 0:nh], heads[:, :, D]).then_inc(y_step, 1)
                    for k in range(nh):
                        dve.wait_ge(y_step, b * (2 * Y_STEPS) + (at + k))
                        stt(xb, heads[:, k, 0:D], y_rc[:, k:k + 1], xb, ALU.mult, ALU.add)\
                            .then_inc(y_step if k < nh - 1 else aux_free, 1)
                elif n == 0:
                    cp(hT[:, :], bank[:, 0:S]).then_inc(aux_free, 1)
                elif n == 1:
                    f_inc(cp(qT[:, :], bank[:, 0:S]), b, "qT")
                    f_inc(cp(v9[:, :, 0:DS], bank[0:S, 2 * P:3 * P].rearrange("p (h d) -> p h d", d=DS)), b, "v")
                    tt(kbd[:, :, :], bank[:, P:P + S].unsqueeze(1).broadcast_to([P, H, S]),
                       head_mask[:, :].unsqueeze(2).broadcast_to([P, H, S]), ALU.mult).then_inc(aux_free, 1)
                elif n < 6:
                    g = n - 2
                    sc = bank[0:S, 0:GW].rearrange("p (k s) -> p k s", s=S)
                    f_inc(v.tensor_reduce(mx4[:, g, :], sc, AX.X, ALU.max), b, f"mx{g}", True)
                    tt(ex[:, g, :, :], sc, mx4[:, g, :].unsqueeze(2).broadcast_to([S, 4, S]),
                       ALU.subtract).then_inc(aux_free, 1)
                elif n < 10:
                    cp(pT[:, n - 6, :], bank[0:S, 0:GW]).then_inc(aux_free, 1)
                elif n == 10:
                    o9 = bank[0:S, 0:H * (DS + 1)].rearrange("p (h d) -> p h d", d=DS + 1)
                    f_inc(v.reciprocal(s_rc[:, :], o9[:, :, DS]), b, "rc", True)
                    tt(sctx[:, :, :], o9[:, :, 0:DS], s_rc[:, :].unsqueeze(2).broadcast_to([S, H, DS]),
                       ALU.mult).then_inc(aux_free, 1)
                elif n == 11:
                    cp(sctxT[:, :], bank[:, 0:S]).then_inc(aux_free, 1)
                elif n == 12:
                    tt(x2[:, bat(b), :].squeeze(1), bank[0:S, 0:D], xf[:, :], ALU.add).then_inc(aux_free, 1)
                else:
                    cp(h2T[:, tok(b)], bank[:, 0:S]).then_inc(aux_free, 1)

            run_aux(aux, PREP, 0, "prep", 0)

            def body(b, kind, parity):
                for i in range(UNITS):
                    run_aux(aux, steps(kind)[0][i], b, kind, parity)
                    probs_rest(b, i)

            batches(dve, body)
            run_aux(aux, LAST, B, "end", 0)

            count = [0]

            def link(ins):
                count[0] += 1
                ins.then_inc(top, 1)
                dve.wait_ge(top, count[0])

            def be(t):
                return t.unsqueeze(2).broadcast_to([S, B, E])

            logits = psum[0:S, ACCB + 1, 0:B * E].rearrange("p (b e) -> p b e", e=E)
            dve.wait_ge(logit_full, 1)
            link(v.tensor_reduce(rt_m[:, :], logits, AX.X, ALU.max))
            link(tt(rt_p[:, :, :], logits, be(rt_m[:, :]), ALU.subtract))
            assert count[0] == T_SUB
            dve.wait_ge(silu_out, 1)
            link(v.tensor_reduce(rt_m[:, :], rt_p[:, :, :], AX.X, ALU.add))
            link(v.reciprocal(rt_m[:, :], rt_m[:, :]))
            link(tt(rt_p[:, :, :], rt_p[:, :, :], be(rt_m[:, :]), ALU.mult))
            for e in range(E):
                link(v.memset(rt_no[:, :, e:e + 1], float(E - e)))
            for s, top_p in ((0, rt_a), (1, rt_b)):
                link(v.tensor_reduce(top_p[:, :], rt_p[:, :, :], AX.X, ALU.max))
                link(tt(rt_s[s][:, :, :], rt_p[:, :, :], be(top_p[:, :]), ALU.is_equal))
                link(tt(rt_s[s][:, :, :], rt_s[s][:, :, :], rt_no[:, :, :], ALU.mult))
                link(v.tensor_reduce(rt_m[:, :], rt_s[s][:, :, :], AX.X, ALU.max))
                link(tt(rt_s[s][:, :, :], rt_no[:, :, :], be(rt_m[:, :]), ALU.is_equal))
                if s == 0:
                    link(stt(rt_p[:, :, :], rt_s[0][:, :, :], -2.0, rt_p[:, :, :], ALU.mult, ALU.add))
            link(tt(rt_e[:, :], rt_b[:, :], rt_a[:, :], ALU.subtract))
            assert count[0] == T_D, count[0]
            dve.wait_ge(silu_out, 2)
            link(ts(rt_a[:, :], rt_e[:, :], 1.0, None, ALU.add))
            link(v.reciprocal(rt_a[:, :], rt_a[:, :]))
            link(tt(rt_b[:, :], rt_a[:, :], rt_e[:, :], ALU.mult))
            link(tt(rt_s[0][:, :, :], rt_s[0][:, :, :], be(rt_a[:, :]), ALU.mult))
            link(tt(rt_s[1][:, :, :], rt_s[1][:, :, :], be(rt_b[:, :]), ALU.mult))
            link(tt(comb[:, :, 0:E], rt_s[0][:, :, :], rt_s[1][:, :, :], ALU.add))
            link(v.memset(comb[:, :, E:E + 1], 1.0))

            def hidden_unit(q, n):
                dve.wait_ge(silu_out, q * EU + (n + 3))
                wait_past(dve, down_full, q * EU + max(n - 2, 0))
                tt(hidden[:, n % 3, :], silu[:, n % 3, :], psum[:, 2 * (n % 2) + 1, 0:GW], ALU.mult).then_inc(hid, 1)

            def add_expert(q, e):
                dve.wait_ge(down_full, q * EU + NF * (e + 1))
                if e:
                    dve.wait_ge(sum2, q * 4 * (E + 1) + 4 * e)
                for k in range(4):
                    xb = x2[:, bat(q * 4 + k), :].squeeze(1)
                    w = comb[:, bat(q * 4 + k), e]
                    stt(xb, psum[0:S, AUXB + e % 2, k * D:(k + 1) * D], w, xb, ALU.mult, ALU.add).then_inc(sum2, 1)

            def group(q):
                for n in range(EU):
                    hidden_unit(q, n)
                    if n >= 3 and n % 2 == 1:
                        add_expert(q, (n - 3) // 2)
                add_expert(q, E)
                dve.wait_ge(sum2, (q + 1) * 4 * (E + 1))
                four = cut(q, 4)
                stt(sqb[:, four, :], x2[:, four, :], tf[0:S, 0:1], x1[:, four, :], ALU.mult, ALU.add).then_inc(fin, 1)

            groups(dve, group)


_INS = ["x", "ctx_768", "g_xattn", "g_ffn", "L0_xattn_w_q", "L0_xattn_w_k", "L0_xattn_w_v", "L0_xattn_w_o",
        "L0_xattn_b_o", "L0_ffn_norm1_w", "L0_ffn_norm2_w", "L0_ffn_wq", "L0_ffn_wk", "L0_ffn_wv", "L0_ffn_wo",
        "L0_ffn_router_w", "L0_ffn_sh_gate", "L0_ffn_sh_up", "L0_ffn_sh_down", "L0_ffn_e_gate", "L0_ffn_e_up",
        "L0_ffn_e_down"]
_OUTS = [((16, 100, 128), "float32")]


def kernel(**inputs):
    import numpy as _np
    import concourse.bacc as _bacc
    from concourse import mybir as _mybir
    from concourse.bass_utils import run_bass_kernel_spmd as _run

    nc = _bacc.Bacc("TRN2", target_bir_lowering=False, num_devices=1)
    arrays, args = {}, []
    for name in _INS:
        a = _np.ascontiguousarray(inputs[name])
        arrays[f"in_{name}_dram"] = a
        args.append(nc.dram_tensor(f"in_{name}_dram", a.shape, _mybir.dt.from_np(a.dtype), kind="ExternalInput").ap())
    for i, (shape, dtype) in enumerate(_OUTS):
        dt = _mybir.dt.from_np(_np.dtype(dtype))
        args.append(nc.dram_tensor(f"out_{i}_dram", shape, dt, kind="ExternalOutput").ap())
    flamingo_kernel(nc, *args)
    r = _run(nc, [arrays], core_ids=[0])
    return r.results[0]["out_0_dram"]
```

```python
from contextlib import ExitStack
from math import log

import concourse.bass as bass
from concourse import mybir

F32 = mybir.dt.float32
F16 = mybir.dt.float16
ALU = mybir.AluOpType
ACT = mybir.ActivationFunctionType
AX = mybir.AxisListType

LN_EPS = 1e-5
RMS_EPS = 1e-6
P = 128


def flamingo_kernel(nc, x, ctx, g_xattn, g_ffn, w_q, w_k, w_v, w_o, b_o, norm1_w, norm2_w,
                    wq, wk, wv, wo, router_w, sh_gate, sh_up, sh_down, e_gate, e_up, e_down, out):
    B, S, D = x.shape
    KV, C = ctx.shape[1:]
    DH = 64
    H = w_q.shape[1] // DH
    DS = D // H
    E, _, F = e_gate.shape
    NF = F // P
    FULL = KV // P
    REM = KV - FULL * P
    CH = FULL + 1
    HALF = H // 2
    GW = 4 * S
    ROWS = H * S
    UNITS = 2 * CH
    RT = -(-ROWS // P)
    MW = 512
    MP = -(-KV // MW)
    SHIFT = 10 * log(2.0) * DH ** 0.5
    YB = [(0, 1, 2), (3, 4, 5), (6, 7)]
    YW = D + 1

    plan = {i: [] for i in range(UNITS)}
    for n, i in enumerate((0, 0, 1)):
        plan[i].append(("t", n))
    for n, i in enumerate((1, 1, 2, 2)):
        plan[i].append(("q", n))
    for n, i in enumerate((3, 4, 5)):
        plan[i].append(("y1", n))
    for n, i in enumerate((15, 16, 17)):
        plan[i].append(("y0", n))
    plan[5].append(("ln", 0))
    plan[7].append(("xf", 0))
    for n, i in enumerate((8, 9, 10, 11, 12, 13, 13, 14, 14, 15, 18, 19, 20, 23)):
        plan[i].append(("f", n))
    plan[20].append(("rs", 0))
    plan[22].append(("h2", 0))
    LO_POOL = (8, 10, 12, 14, 16, 18)
    NPU = RT * MP
    F_LOAD = {0: .3, 1: 2.1, 6: 0, 7: 0, 8: 0, 9: 0, 10: .6, 11: .3, 12: .3, 13: .3}
    LOAD = {"t": .7, "q": .6, "y0": .9, "y1": .9, "ln": .5, "xf": .4, "rs": .5, "h2": .2}
    load = {i: sum(F_LOAD.get(u[1], 1.1) if u[0] == "f" else LOAD[u[0]] for u in plan[i]) for i in plan}
    for i in plan:
        load[i] += 0 if i - 1 in LO_POOL else .9
    share = {i: 0 for i in range(3, 21)}
    for n in range(NPU):
        i = min(share, key=lambda i: (load[i], i))
        share[i] += 1
        load[i] += .6
    n = 0
    for i in share:
        for _ in range(share[i]):
            plan[i].append(("p", n))
            n += 1
    plan[21].append(("m", 0))
    PREP = [("t", n) for n in range(3)] + [("q", n) for n in range(4)] + \
           [("p", n) for n in range(NPU)] + [("m", 0)]
    LAST = [("y1", n) for n in range(3)] + [("ln", 0), ("xf", 0)] + [("f", n) for n in range(13)] + \
           [("rs", 0), ("h2", 0), ("f", 13)]
    NO_BANK = ("ln", "xf", "rs", "h2")
    KINDS_FIRST = ("y0", "t", "q", "p", "m")
    KINDS_LAST = ("y0", "y1", "f") + NO_BANK
    flat = [u for i in range(UNITS) for u in plan[i] if u[0] not in NO_BANK]
    A = len(flat)
    A_FIRST = sum(u[0] in KINDS_FIRST for u in flat)
    A_LAST = sum(u[0] in KINDS_LAST for u in flat)
    AT_FIRST = len(PREP)
    AT_LOOP = AT_FIRST + A_FIRST

    END = AT_LOOP + A * (B - 2) + A_LAST
    TOTAL = END + sum(u[0] not in NO_BANK for u in LAST)

    def by_act(u):
        return u[0] == "f" and 6 <= u[1] < 10

    def numbered(units):
        k, free, at = 0, 0, {}
        for u in units:
            at[u] = k, free
            k += u[0] not in NO_BANK
            free += u[0] not in NO_BANK and not by_act(u)
        return at

    def steps(kind):
        kinds = {"first": KINDS_FIRST, "last": KINDS_LAST}.get(kind)
        by_place = [[u for u in plan[i] if kinds is None or u[0] in kinds] for i in range(UNITS)]
        at = numbered([u for us in by_place for u in us])
        thirds = [[us[len(us) * k // 3:len(us) * (k + 1) // 3] for k in range(3)] for us in by_place]
        return thirds, at

    def aux_base(b, kind):
        fixed = {"prep": (0, 0), "first": (AT_FIRST, AT_FIRST), "end": (END, END - 4 * (B - 2) - 4)}
        return fixed.get(kind) or ((b - 1) * A + AT_LOOP, (b - 1) * (A - 4) + AT_LOOP)

    ODD = {"prep": 0, "first": AT_FIRST % 2, "odd": AT_LOOP % 2, "even": (AT_LOOP + A) % 2,
           "last": (AT_LOOP + A * (B - 2)) % 2, "end": END % 2}

    def batch_of(unit, b):
        return b + {"t": 1, "q": 1, "p": 1, "m": 1, "y0": 0}.get(unit[0], -1)

    F_STEPS = ["stats", "aggr", "xf", "h", "qT", "v", "mx0", "mx1", "mx2", "mx3", "rc",
               "stats2", "aggr2", "h2"]
    NFS = len(F_STEPS)
    P_STEPS = ["var+eps", "rstd", "rstd2", "ms", "ms+eps", "r", "rr", "mean2", "ms2", "ms2+eps", "r2"]
    NPS = len(P_STEPS)
    SET_POOL = ["-1/2", "zero ident", "ident", "zero ident16", "ident16", "lnr", "Nh right", "Nh below",
                "Nh corner", "ones cT0", "pad c_hi0", "ones c_hi0", "pad c_lo0", "ones cT1", "pad c_hi1",
                "ones c_hi1", "pad c_lo1", "mx", "ones v9", "ones mask", "mask above", "head_mask",
                "n1", "wg", "wu", "rw"]
    SET_DVE = ["sum", "mean", "centred", "square", "sumsq", "lnvar", "xln", "bot", "wqT", "wkT", "wvT",
               "xlnT0", "xlnT1", "Mh0", "Mh1", "Nh0", "Nh1", "xlnT2", "xlnT3", "x1"]
    SET_PE = ["wqT", "wkT", "wvT", "xlnT0", "xlnT1", "Mh", "Nh", "xlnT2", "xlnT3"]
    Y_STEPS = 8
    EU = (E + 1) * NF

    with ExitStack() as stack:
        def sb(name, shape, dt=F32):
            return stack.enter_context(nc.sbuf_tensor(name, shape, dt))

        def sem(name):
            return stack.enter_context(nc.semaphore(name))

        ident = sb("ident", [P, P])
        ident16 = sb("ident16", [P, P], F16)
        head_mask = sb("head_mask", [P, H])
        minus_half = sb("minus_half", [P, H])
        x1 = sb("x1", [S, B, D])
        x2 = sb("x2", [S, B, D])
        xlnT = sb("xlnT", [D, B * S])
        h2T = sb("h2T", [D, B * S])
        Mh = sb("Mh", [D, H, C])
        Nh = sb("Nh", [C + 1, H, YW])
        ctx_nat = sb("ctx_nat", [P, CH, C])
        c_hi = [sb(f"c_hi{q}", [P, CH, P], F16) for q in range(2)]
        c_lo = [sb(f"c_lo{q}", [P, CH, P], F16) for q in range(2)]
        cT_hi = [sb(f"cT_hi{q}", [C + 1, KV], F16) for q in range(2)]
        cT_lo = [sb(f"cT_lo{q}", [C, KV], F16) for q in range(2)]
        qk_hi = [sb(f"qk_hi{q}", [C + 1, ROWS], F16) for q in range(2)]
        qk_lo = [sb(f"qk_lo{q}", [C, ROWS], F16) for q in range(2)]
        p32 = sb("p32", [P, 3, 2, GW])
        p_hi = sb("p_hi", [P, 3, 2, GW], F16)
        p_lo = sb("p_lo", [P, 3, 2, GW], F16)
        acc_sb = [sb(f"acc_sb{g}", [C + 1, 2, GW]) for g in range(2)]
        mx = sb("mx", [P, RT, MP])
        mx_row = sb("mx_row", [P, RT])
        mneg = sb("mneg", [P, RT], F16)
        mrow = sb("mrow", [RT, P], F16)
        y_rc = sb("y_rc", [S, 3])
        n1 = sb("n1", [D, 1])
        n2 = sb("n2", [D, 1])
        sw = sb("sw", [D, 4, D])
        stats = sb("stats", [S, 6])
        aggr = sb("aggr", [S, 2])
        stats2 = sb("stats2", [S, 6])
        aggr2 = sb("aggr2", [S, 2])
        ps = sb("ps", [S, NPS])
        xf = sb("xf", [S, D])
        hn = sb("hn", [S, D])
        hT = sb("hT", [D, S])
        qT = sb("qT", [D, S])
        kbd = sb("kbd", [D, H, S])
        v9 = sb("v9", [S, H, DS + 1])
        mx4 = sb("mx4", [S, 4, 4])
        ex = sb("ex", [S, 4, 4, S])
        pT = sb("pT", [S, 4, GW])
        s_rc = sb("s_rc", [S, H])
        sctx = sb("sctx", [S, H, DS])
        sctxT = sb("sctxT", [D, S])
        hn2 = sb("hn2", [S, D])
        wg = sb("wg", [D, E + 1, F])
        wu = sb("wu", [D, E + 1, F])
        wd = sb("wd", [P, E + 1, NF, D])
        rw = sb("rw", [D, E])
        gx = sb("gx", [P, 1])
        gf = sb("gf", [P, 1])
        tx = sb("tx", [P, 1])
        tf = sb("tf", [P, 1])
        bo = sb("bo", [S, D])

        psum = stack.enter_context(nc.psum_tensor("psum", [P, 8, 512], F32))
        ACCB, AUXB = 4, 6

        names = ["w_in", "e_in", "set_pool", "set_dve", "set_act", "set_pe",
                 "ctx_in", "row_in", "split", "scores", "probs_hi", "probs_lo", "pv", "acc_out",
                 "aux_full", "aux_free", "hi_out", "max_step", "y_step", "f_step", "pool_step",
                 "exp_out", "pt_out", "lo_pool", "logit_full", "top", "gu_full", "silu_out", "hid", "down_full", "sum2",
                 "fin", "out_done"]
        sm = {n: sem(n) for n in names}
        w_in, e_in, set_pool, set_dve, set_act, set_pe = (sm[n] for n in names[:6])
        ctx_in, row_in, split, scores, probs_hi, probs_lo, pv, acc_out = (sm[n] for n in names[6:14])
        aux_full, aux_free, hi_out, max_step, y_step, f_step, pool_step = (sm[n] for n in names[14:21])
        exp_out, pt_out, lo_pool, logit_full, top, gu_full, silu_out, hid, down_full, sum2, fin, out_done = \
            (sm[n] for n in names[21:])

        def f_at(c, name):
            return c * NFS + (F_STEPS.index(name) + 1)

        def p_at(c, name):
            return c * NPS + (P_STEPS.index(name) + 1)

        def pcol(name):
            k = P_STEPS.index(name)
            return ps[:, k:k + 1]

        def lo_made(b, i):
            if i < 0:
                return lo_made(b - 1, i + UNITS)
            by_pool = sum(u < i for u in LO_POOL)
            if i in LO_POOL:
                return lo_pool, b * len(LO_POOL) + (by_pool + 1)
            return probs_lo, b * (UNITS - len(LO_POOL)) + (i - by_pool + 1)

        def set_wait(eng, signal, order, name):
            eng.wait_ge(signal, order.index(name) + 1)

        def wait_apart(eng, signal, value):
            if not isinstance(value, int):
                value = eng.to_reg(value)
                eng.wait_ge(w_in, 16)
            eng.wait_ge(signal, value)

        def batches(eng, body):
            body(0, "first", 0)
            with eng.Fori(0, (B - 2) // 2) as r:
                body(r * 2 + 1, "odd", 1)
                body(r * 2 + 2, "even", 0)
            body(B - 1, "last", 1)

        def groups(eng, body):
            body(0)
            with eng.Fori(1, B // 4) as q:
                body(q)

        def wait_past(eng, signal, value):
            if not (isinstance(value, int) and value == 0):
                eng.wait_ge(signal, value)

        def run_aux(aux, units, b, kind, parity):
            at = {"prep": numbered(PREP), "end": numbered(LAST)}.get(kind) or steps(kind)[1]
            base = aux_base(b, kind)
            order = [u for u in at if u[0] not in NO_BANK]
            for u in units:
                on = 0 if kind == "prep" else batch_of(u, b)
                near = 0 if kind == "prep" else batch_of(u, 0)
                k, free = at[u]
                last = order[k - 2] if k >= 2 else None
                last_free = at[last][1] + 1 if last else k - 1
                aux(base[0] + k, base[1] + free, (ODD[kind] + k) % 2, u, on, (parity + near) % 2,
                    lambda other: base[1] + at[other][1] + 1,
                    (pt_out, batch_of(last, b) * 4 + (last[1] - 5)) if last and by_act(last)
                    else (aux_free, base[1] + last_free))

        def cut(q, n):
            return slice(q * n, q * n + n) if isinstance(q, int) else bass.ds(q * n, n)

        def tok(b):
            return slice(b * S, b * S + S) if isinstance(b, int) else bass.ds(b * S, S)

        def bat(b, n=1):
            return slice(b, b + n) if isinstance(b, int) else bass.ds(b, n)

        def kc(j):
            m = P if j < FULL else REM
            return slice(j * P, j * P + m), m

        def rows_of(t):
            return min(P, ROWS - t * P)

        NSPLIT = 4
        W_LOADS, E_LOADS = 13, 2 * 2 + E + 1 + 2
        T_SUB, T_D = 2, 2 + 3 + E + 11 + 1

        wq_nat = p32[:, :, :, :].rearrange("p a k w -> p (a k w)")[:, 0:H * DH]
        wk_nat = sb("wk_nat", [C, H * DH])
        wv_nat = sb("wv_nat", [C, H * DH])
        wo_nat = sb("wo_nat", [P, H // 2, D])
        wqT = sb("wqT", [P, H // 2, D])
        wkT = sb("wkT", [P, H // 2, C])
        wvT = sb("wvT", [P, H // 2, C])
        xc = x2
        lnsum = sb("lnsum", [S, B])
        lnvar = sb("lnvar", [S, B])
        lnr = sb("lnr", [S, B])
        bot = sb("bot", [S, D])
        sqb = sb("sqb", [S, B, D])
        rt_m = sb("rt_m", [S, B])
        rt_a = sb("rt_a", [S, B])
        rt_b = sb("rt_b", [S, B])
        rt_e = sb("rt_e", [S, B])
        rt_p = sb("rt_p", [S, B, E])
        rt_no = sb("rt_no", [S, B, E])
        rt_s = [sb(f"rt_s{k}", [S, B, E]) for k in range(2)]
        comb = sb("comb", [S, B, E + 1])
        silu = p32[:, :, 0, :]
        hidden = p32[:, :, 1, :]

        def probs_rest(eng, engine, b, i):
            m = kc(i % CH)[1]
            eng.wait_ge(probs_hi, b * UNITS + (i + 1))
            if not (isinstance(b, int) and b == 0 and i < 3):
                eng.wait_ge(pv, b * UNITS + (i - 2))
            engine.tensor_tensor(p_lo[0:m, i % 3, :, :], p32[0:m, i % 3, :, :], p_hi[0:m, i % 3, :, :],
                                 ALU.subtract).then_inc(lo_made(b, i)[0], 1)

        block = stack.enter_context(nc.Block())

        @block.sync
        def _(sp):
            def load(dst, src, signal=w_in):
                sp.dma_start(dst, src).then_inc(signal, 16)

            def load_ctx(b):
                sp.dma_start(ctx_nat[:, 0:FULL, :], ctx[bat(b), 0:FULL * P, :].rearrange(
                    "b (p j) c -> p (b j) c", j=FULL)).then_inc(ctx_in, 16)
                sp.dma_start(ctx_nat[0:REM, FULL, :], ctx[bat(b), FULL * P:KV, :].rearrange(
                    "b r c -> (b r) c")).then_inc(ctx_in, 16)

            def send_row(b, parity, free):
                sp.wait_ge(aux_free, free + 1)
                sp.dma_start(qk_hi[parity][C:C + 1, 0:(RT - 1) * P], mrow[0:RT - 1, :]).then_inc(row_in, 16)
                sp.dma_start(qk_hi[parity][C:C + 1, (RT - 1) * P:ROWS],
                             mrow[RT - 1:RT, 0:rows_of(RT - 1)]).then_inc(row_in, 16)

            load(x1[:, :, :], x.rearrange("b s d -> s b d"))
            load_ctx(0)
            load(wq_nat, w_q)
            load(wk_nat[:, :], w_k)
            load(wv_nat[:, :], w_v)
            load(wo_nat[:, :, :], w_o.rearrange("(a k) d -> k a d", k=P))
            load(gx[:, :], g_xattn.partition_broadcast(P))
            load(gf[:, :], g_ffn.partition_broadcast(P))
            load(bo[:, :], b_o.partition_broadcast(S))
            load(n1[:, :], norm1_w.rearrange("(p a) -> p a", a=1))
            for k, w in enumerate((wq, wk, wv, wo)):
                load(sw[:, k, :], w)
            load(n2[:, :], norm2_w.rearrange("(p a) -> p a", a=1), e_in)
            load(rw[:, :], router_w, e_in)
            for dst, many, one in ((wg, e_gate, sh_gate), (wu, e_up, sh_up)):
                load(dst[:, 0:E, :], many.rearrange("e d f -> d e f"), e_in)
                load(dst[:, E, :], one, e_in)
            for e in range(E):
                load(wd[:, e, :, :], e_down[e].rearrange("(a p) d -> p a d", p=P), e_in)
            load(wd[:, E, :, :], sh_down.rearrange("(a p) d -> p a d", p=P), e_in)

            def load_after(b):
                sp.wait_ge(hi_out, b * 7 + 3)
                sp.wait_ge(split, (b + 1) * NSPLIT)
                load_ctx(b + 1)

            def row_of(b, kind, parity):
                if kind != "first":
                    sp.wait_ge(scores, b * UNITS)
                send_row(b + 1, 1 - parity, aux_base(b, kind)[1] + steps(kind)[1][("m", 0)][1])

            load_after(0)
            send_row(0, 0, len(PREP) - 1)
            load_after(1)
            row_of(0, "first", 0)
            with sp.Fori(0, (B - 4) // 2) as r:
                for b, kind, parity in ((r * 2 + 1, "odd", 1), (r * 2 + 2, "even", 0)):
                    load_after(b + 1)
                    row_of(b, kind, parity)
            load_after(B - 2)
            row_of(B - 3, "odd", 1)
            row_of(B - 2, "even", 0)
            for q in range(4):
                sp.wait_ge(fin, q + 1)
                sp.dma_start(out[4 * q:4 * q + 4].rearrange("b s d -> s b d"),
                             sqb[:, 4 * q:4 * q + 4, :]).then_inc(out_done, 16)
            sp.wait_ge(out_done, 64)

        @block.gpsimd
        def _(pool):
            g = nc.gpsimd

            def step(name, ins):
                ins.then_inc(set_pool, 1)
                set_wait(pool, set_pool, SET_POOL, name)

            def select(t, base, pattern, cm, op, fill):
                return g.affine_select(out=t[:, :], in_=t[:, :], compare_op=op, fill=fill, base=base,
                                       pattern=pattern, channel_multiplier=cm)

            step("-1/2", g.memset(minus_half[:, :], -0.5))
            step("zero ident", g.memset(ident[:, :], 0.0))
            step("ident", select(ident, 0, [[-1, P]], 1, ALU.not_equal, 1.0))
            step("zero ident16", g.memset(ident16[:, :], 0.0))
            step("ident16", select(ident16, 0, [[-1, P]], 1, ALU.not_equal, 1.0))
            set_wait(pool, set_dve, SET_DVE, "lnvar")
            step("lnr", g.tensor_tensor(lnr[:, :], lnvar[:, :], minus_half[0:S, :], ALU.pow))
            step("Nh right", g.memset(Nh[:, :, D:YW], 0.0))
            step("Nh below", g.memset(Nh[C:C + 1, :, 0:D], 0.0))
            step("Nh corner", g.memset(Nh[C:C + 1, :, D:YW], 1.0))
            for q in range(2):
                step(f"ones cT{q}", g.memset(cT_hi[q][C:C + 1, :], 1.0))
                step(f"pad c_hi{q}", g.memset(c_hi[q][:, :, C:P], 0.0))
                step(f"ones c_hi{q}", g.memset(c_hi[q][:, :, C:C + 1], 1.0))
                step(f"pad c_lo{q}", g.memset(c_lo[q][:, :, C:P], 0.0))
            step("mx", g.memset(mx[:, :, :], 0.0))
            step("ones v9", g.memset(v9[:, :, DS:DS + 1], 1.0))
            step("ones mask", g.memset(head_mask[:, :], 1.0))
            step("mask above", select(head_mask, 0, [[-DS, H]], 1, ALU.is_ge, 0.0))
            step("head_mask", select(head_mask, DS - 1, [[DS, H]], -1, ALU.is_ge, 0.0))

            def split_ctx(b, kind, parity):
                wait_apart(pool, ctx_in, (b + 1) * 32)
                if kind not in ("prep", "first"):
                    wait_apart(pool, pv, (b - 1) * UNITS)
                for n, (r, js) in enumerate(((P, slice(0, FULL)), (REM, slice(FULL, CH)))):
                    g.tensor_copy(c_hi[parity][0:r, js, 0:C], ctx_nat[0:r, js, :]).then_inc(split, 1)
                    pool.wait_ge(split, b * NSPLIT + (2 * n + 1))
                    g.tensor_tensor(c_lo[parity][0:r, js, 0:C], ctx_nat[0:r, js, :],
                                    c_hi[parity][0:r, js, 0:C], ALU.subtract).then_inc(split, 1)

            def small(c, name, ins):
                ins.then_inc(pool_step, 1)
                wait_apart(pool, pool_step, p_at(c, name))

            half = minus_half[0:S, 0:1]

            def norm_1(c):
                var = aggr[:, 1:2]
                wait_apart(pool, f_step, f_at(c, "aggr"))
                small(c, "var+eps", g.tensor_scalar(pcol("var+eps"), var, LN_EPS, None, ALU.add))
                small(c, "rstd", g.tensor_tensor(pcol("rstd"), pcol("var+eps"), half, ALU.pow))
                small(c, "rstd2", g.tensor_tensor(pcol("rstd2"), pcol("rstd"), pcol("rstd"), ALU.mult))
                small(c, "ms", g.tensor_tensor(pcol("ms"), pcol("rstd2"), var, ALU.mult))
                small(c, "ms+eps", g.tensor_scalar(pcol("ms+eps"), pcol("ms"), RMS_EPS, None, ALU.add))
                small(c, "r", g.tensor_tensor(pcol("r"), pcol("ms+eps"), half, ALU.pow))
                small(c, "rr", g.tensor_tensor(pcol("rr"), pcol("r"), pcol("rstd"), ALU.mult))

            def norm_2(c):
                pool.wait_ge(f_step, f_at(c, "aggr2"))
                small(c, "mean2", g.tensor_tensor(pcol("mean2"), aggr2[:, 0:1], aggr2[:, 0:1], ALU.mult))
                small(c, "ms2", g.tensor_tensor(pcol("ms2"), pcol("mean2"), aggr2[:, 1:2], ALU.add))
                small(c, "ms2+eps", g.tensor_scalar(pcol("ms2+eps"), pcol("ms2"), RMS_EPS, None, ALU.add))
                small(c, "r2", g.tensor_tensor(pcol("r2"), pcol("ms2+eps"), half, ALU.pow))

            split_ctx(0, "prep", 0)
            step("n1", g.tensor_scalar(sw[:, 0:3, :], sw[:, 0:3, :], n1[:, 0:1], None, ALU.mult))
            pool.wait_ge(e_in, 16 * E_LOADS)
            for name, w in (("wg", wg[:, :, :]), ("wu", wu[:, :, :]), ("rw", rw[:, :])):
                step(name, g.tensor_scalar(w, w, n2[:, 0:1], None, ALU.mult))

            def body(b, kind, parity):
                if kind != "last":
                    split_ctx(b + 1, kind, 1 - parity)
                if kind != "first":
                    norm_1(b - 1)
                for i in LO_POOL:
                    probs_rest(pool, g, b, i)
                if kind != "first":
                    norm_2(b - 1)

            batches(pool, body)
            norm_1(B - 1)
            norm_2(B - 1)

        @block.tensor
        def _(pe):
            mm = nc.tensor.matmul
            tr = nc.tensor.transpose

            pe.wait_ge(w_in, 16 * W_LOADS)
            set_wait(pe, set_pool, SET_POOL, "ident16")
            for a in range(H // 2):
                t = tr(psum[:, a // 4, (a % 4) * D:(a % 4) * D + D], wq_nat[:, a * P:(a + 1) * P], ident[:, :])
            t.then_inc(set_pe, 1)
            for k, w in enumerate((wk_nat, wv_nat)):
                for a in range(H // 2):
                    t = tr(psum[:, 2 + 2 * k + a // 4, (a % 4) * C:(a % 4) * C + C],
                           w[:, a * P:(a + 1) * P], ident[0:C, 0:C])
                t.then_inc(set_pe, 1)
            set_wait(pe, set_dve, SET_DVE, "xln")
            for g in range(2):
                for k in range(4):
                    t = tr(psum[:, AUXB + g, k * S:(k + 1) * S], xc[:, 4 * g + k, :], ident[0:S, 0:S])
                t.then_inc(set_pe, 1)
            set_wait(pe, set_dve, SET_DVE, "wkT")
            for r in range(2):
                for a in range(H // 2):
                    rs = slice(DH * r, DH * r + DH)
                    t = mm(psum[:, 2 * r + a // 4, (a % 4) * C:(a % 4) * C + C], wqT[rs, a, :], wkT[rs, a, :],
                           start=True, stop=True)
            t.then_inc(set_pe, 1)
            set_wait(pe, set_dve, SET_DVE, "xlnT1")
            for r in range(2):
                for a in range(H // 2):
                    rs = slice(DH * r, DH * r + DH)
                    t = mm(psum[0:C, 4 + 2 * r + a // 4, (a % 4) * D:(a % 4) * D + D], wvT[rs, a, :],
                           wo_nat[rs, a, :], start=True, stop=True)
            t.then_inc(set_pe, 1)
            set_wait(pe, set_dve, SET_DVE, "Mh1")
            for g in range(2, 4):
                for k in range(4):
                    t = tr(psum[:, g - 2, k * S:(k + 1) * S], xc[:, 4 * g + k, :], ident[0:S, 0:S])
                t.then_inc(set_pe, 1)
            set_wait(pe, set_dve, SET_DVE, "xlnT3")

            set_wait(pe, set_pool, SET_POOL, "head_mask")

            def score_unit(b, parity, i):
                g, j = divmod(i, CH)
                cols, m = kc(j)
                if isinstance(b, int) and b == 0 and i < 2:
                    pass
                else:
                    pe.wait_ge(probs_hi, b * UNITS + (i - 1))
                if i == 0:
                    pe.wait_ge(row_in, (b + 1) * 32)
                s = i % 2
                outs = [psum[0:m, 2 * s + k, 0:GW] for k in range(2)]
                qs = [slice((2 * g + k) * GW, (2 * g + k + 1) * GW) for k in range(2)]
                for k in range(2):
                    mm(outs[k], cT_hi[parity][:, cols], qk_hi[parity][:, qs[k]], start=True, stop=False)
                for k in range(2):
                    mm(outs[k], cT_hi[parity][0:C, cols], qk_lo[parity][:, qs[k]], start=False, stop=False)
                for k in range(2):
                    t = mm(outs[k], cT_lo[parity][:, cols], qk_hi[parity][0:C, qs[k]], start=False, stop=True)
                t.then_inc(scores, 1)

            def pv_unit(b, parity, i, between=lambda: None):
                j = i % CH
                m = kc(j)[1]
                pe.wait_ge(*lo_made(b, i))
                if i == 0:
                    pe.wait_ge(split, (b + 1) * NSPLIT)
                if j == 0 and not (isinstance(b, int) and b == 0 and i == 0):
                    pe.wait_ge(acc_out, b * 2 + i // CH)
                outs = [psum[:, ACCB + k, 0:GW] for k in range(2)]
                for w, p in ((c_hi, p_hi), (c_hi, p_lo), (c_lo, p_hi)):
                    for k in range(2):
                        t = mm(outs[k], w[parity][0:m, j, :], p[0:m, i % 3, k, :],
                               start=(j == 0 and w is c_hi and p is p_hi), stop=(j == CH - 1 and w is c_lo))
                    if w is c_hi and p is p_lo:
                        between()
                t.then_inc(pv, 1)

            def aux(seq, free, par, unit, b, parity, out_of, last):
                kind, n = unit
                if kind in NO_BANK:
                    return
                if not (isinstance(seq, int) and seq < 2):
                    pe.wait_ge(*last)
                bank = psum[:, AUXB + par, :]
                if kind == "t":
                    if n == 0:
                        pe.wait_ge(ctx_in, (b + 1) * 32)
                    for k in range(4):
                        m = kc(4 * n + k)[1]
                        t = tr(bank[0:C, k * P:k * P + m], ctx_nat[0:m, 4 * n + k, :], ident[0:m, 0:m])
                elif kind == "q":
                    for k in range(4):
                        t = mm(bank[0:C, k * S:(k + 1) * S], Mh[:, 4 * n + k, :], xlnT[:, tok(b)],
                               start=True, stop=True)
                elif kind == "p":
                    rt, part = divmod(n, MP)
                    if n == 0:
                        pe.wait_ge(aux_free, free)
                    r = rows_of(rt)
                    w = min(MW, KV - part * MW)
                    t = mm(bank[0:r, 0:w], qk_hi[parity][0:C, rt * P:rt * P + r],
                           cT_hi[parity][0:C, part * MW:part * MW + w], start=True, stop=True)
                elif kind == "m":
                    pe.wait_ge(max_step, (b + 1) * 2)
                    t = tr(bank[0:RT, 0:P // 2].bitcast(F16), mneg[:, :], ident16[:, :])
                elif kind in ("y0", "y1"):
                    half = int(kind[1])
                    if n == 0:
                        pe.wait_ge(acc_out, b * 2 + (half + 1))
                    for k, h in enumerate(YB[n]):
                        t = mm(bank[0:S, k * YW:(k + 1) * YW], acc_sb[half][:, h // 4, (h % 4) * S:(h % 4 + 1) * S],
                               Nh[:, half * HALF + h, :], start=True, stop=True)
                elif n == 0:
                    pe.wait_ge(f_step, f_at(b, "h"))
                    t = tr(bank[:, 0:S], hn[:, :], ident[0:S, 0:S])
                elif n == 1:
                    pe.wait_ge(aux_free, out_of(("f", 0)))
                    mm(bank[:, 0:S], sw[:, 0, :], hT[:, :], start=True, stop=True)
                    mm(bank[:, P:P + S], sw[:, 1, :], hT[:, :], start=True, stop=True)
                    t = mm(bank[0:S, 2 * P:3 * P], hT[:, :], sw[:, 2, :], start=True, stop=True)
                elif n < 6:
                    if n == 2:
                        pe.wait_ge(aux_free, out_of(("f", 1)))
                    t = mm(bank[0:S, 0:GW], qT[:, :], kbd[:, 4 * (n - 2):4 * (n - 1), :].rearrange("p a s -> p (a s)"),
                           start=True, stop=True)
                elif n < 10:
                    pe.wait_ge(exp_out, b * 4 + (n - 5))
                    for k in range(4):
                        t = tr(bank[0:S, k * S:(k + 1) * S], ex[:, n - 6, k, :], ident[0:S, 0:S])
                elif n == 10:
                    pe.wait_ge(pt_out, b * 4 + 4)
                    for h in range(H):
                        t = mm(bank[0:S, h * (DS + 1):(h + 1) * (DS + 1)], pT[:, h // 4, (h % 4) * S:(h % 4 + 1) * S],
                               v9[:, h, :], start=True, stop=True)
                elif n == 11:
                    pe.wait_ge(aux_free, out_of(("f", 10)))
                    t = tr(bank[:, 0:S], sctx[:, :, :].rearrange("p h d -> p (h d)"), ident[0:S, 0:S])
                elif n == 12:
                    pe.wait_ge(aux_free, out_of(("f", 11)))
                    t = mm(bank[0:S, 0:D], sctxT[:, :], sw[:, 3, :], start=True, stop=True)
                else:
                    pe.wait_ge(f_step, f_at(b, "h2"))
                    t = tr(bank[:, 0:S], hn2[:, :], ident[0:S, 0:S])
                t.then_inc(aux_full, 1)

            run_aux(aux, PREP, 0, "prep", 0)

            def body(b, kind, parity):
                for i in range(UNITS):
                    score_unit(b, parity, i)
                    one, two, three = steps(kind)[0][i]
                    run_aux(aux, one, b, kind, parity)

                    def middle():
                        run_aux(aux, two, b, kind, parity)

                    if i >= 2:
                        pv_unit(b, parity, i - 2, middle)
                    elif kind != "first":
                        pv_unit(b - 1, 1 - parity, UNITS - 2 + i, middle)
                    else:
                        middle()
                    run_aux(aux, three, b, kind, parity)

            batches(pe, body)
            for i in (UNITS - 2, UNITS - 1):
                pv_unit(B - 1, 1, i)
            run_aux(aux, LAST, B, "end", 0)

            pe.wait_ge(aux_free, TOTAL - 4 * (B - 1) - 4)
            set_wait(pe, set_pool, SET_POOL, "rw")
            for b in range(B):
                t = mm(psum[0:S, ACCB + 1, b * E:(b + 1) * E], h2T[:, tok(b)], rw[:, :], start=True, stop=True)
            t.then_inc(logit_full, 1)

            def gate_up(q, n):
                e, f = divmod(n, NF)
                wait_past(pe, hid, q * EU + max(n - 1, 0))
                for k, w in enumerate((wg, wu)):
                    t = mm(psum[:, 2 * (n % 2) + k, 0:GW], w[:, e, f * P:(f + 1) * P], h2T[:, cut(q, GW)],
                           start=True, stop=True)
                t.then_inc(gu_full, 1)

            def down(q, n):
                e, f = divmod(n, NF)
                pe.wait_ge(hid, q * EU + (n + 1))
                if f == 0 and e >= 2:
                    pe.wait_ge(sum2, q * 4 * (E + 1) + 4 * (e - 1))
                elif f == 0:
                    wait_past(pe, sum2, q * 4 * (E + 1))
                for k in range(4):
                    t = mm(psum[0:S, AUXB + e % 2, k * D:(k + 1) * D], hidden[:, n % 3, k * S:(k + 1) * S],
                           wd[:, e, f, :], start=(f == 0 and k == 0), stop=(f == NF - 1 and k == 3),
                           skip_group_check=True)
                t.then_inc(down_full, 1)

            def group(q):
                for n in range(EU + 2):
                    if n < EU:
                        gate_up(q, n)
                    if n >= 2:
                        down(q, n - 2)

            groups(pe, group)

        @block.scalar
        def _(act):
            a = nc.scalar.activation
            act.wait_ge(w_in, 16 * W_LOADS)
            a(tx[:, :], gx[:, :], ACT.Tanh).then_inc(set_act, 1)
            a(tf[:, :], gf[:, :], ACT.Tanh).then_inc(set_act, 1)

            def evac_hi(seq, par, unit, parity):
                kind, n = unit
                act.wait_ge(aux_full, seq + 1)
                if kind == "t":
                    w = min(512, KV - 512 * n)
                    a(cT_hi[parity][0:C, 512 * n:512 * n + w], psum[0:C, AUXB + par, 0:w], ACT.Copy).then_inc(hi_out, 1)
                else:
                    a(qk_hi[parity][0:C, GW * n:GW * (n + 1)], psum[0:C, AUXB + par, 0:GW], ACT.Copy).then_inc(hi_out, 1)

            def probs(b, i):
                m = kc(i % CH)[1]
                act.wait_ge(scores, b * UNITS + (i + 1))
                if not (isinstance(b, int) and b == 0 and i < 3):
                    act.wait_ge(*lo_made(b, i - 3))
                    act.wait_ge(pv, b * UNITS + (i - 2))
                src = psum[0:m, 2 * (i % 2):2 * (i % 2) + 2, 0:GW]
                a(p32[0:m, i % 3, :, :], src, ACT.Exp, scale=DH ** -0.5)
                a(p_hi[0:m, i % 3, :, :], src, ACT.Exp, scale=DH ** -0.5).then_inc(probs_hi, 1)

            def acc_evac(b, half):
                act.wait_ge(pv, b * UNITS + (half + 1) * CH)
                a(acc_sb[half][:, :, :], psum[0:C + 1, ACCB:ACCB + 2, 0:GW], ACT.Copy).then_inc(acc_out, 1)

            def self_exp(free, c, g):
                act.wait_ge(aux_free, free + 1)
                a(ex[:, g, :, :], ex[:, g, :, :], ACT.Exp, scale=DS ** -0.5).then_inc(exp_out, 1)

            def aux(seq, free, par, unit, b, parity, out_of, last):
                if unit[0] in ("t", "q"):
                    evac_hi(seq, par, unit, parity)
                elif unit[0] == "f" and 2 <= unit[1] < 6:
                    self_exp(free, b, unit[1] - 2)
                elif by_act(unit):
                    act.wait_ge(aux_full, seq + 1)
                    a(pT[:, unit[1] - 6, :], psum[0:S, AUXB + par, 0:GW], ACT.Copy).then_inc(pt_out, 1)

            run_aux(aux, PREP, 0, "prep", 0)

            def body(b, kind, parity):
                for i in range(UNITS):
                    probs(b, i)
                    if i == 2 and kind not in ("first", "last"):
                        act.wait_ge(scores, b * UNITS)
                    for third in steps(kind)[0][i]:
                        run_aux(aux, third, b, kind, parity)
                    if i == 1 and kind != "first":
                        acc_evac(b - 1, 1)
                    if i == CH + 1:
                        acc_evac(b, 0)

            batches(act, body)
            acc_evac(B - 1, 1)
            run_aux(aux, LAST, B, "end", 0)

            act.wait_ge(top, T_SUB)
            a(rt_p[:, :, :], rt_p[:, :, :], ACT.Exp).then_inc(silu_out, 1)
            act.wait_ge(top, T_D)
            a(rt_e[:, :], rt_e[:, :], ACT.Exp).then_inc(silu_out, 1)
            def group(q):
                for n in range(EU):
                    act.wait_ge(gu_full, q * EU + (n + 1))
                    wait_past(act, hid, q * EU + max(n - 2, 0))
                    a(silu[:, n % 3, :], psum[:, 2 * (n % 2), 0:GW], ACT.Silu).then_inc(silu_out, 1)

            groups(act, group)

        @block.vector
        def _(dve):
            v = nc.vector
            tt, ts, stt, cp = v.tensor_tensor, v.tensor_scalar, v.scalar_tensor_tensor, v.tensor_copy

            def step(name, ins, wait=True):
                ins.then_inc(set_dve, 1)
                if wait:
                    set_wait(dve, set_dve, SET_DVE, name)

            def per_token(t):
                return t.unsqueeze(2).broadcast_to([S, B, D])

            dve.wait_ge(w_in, 16 * W_LOADS)
            step("sum", v.tensor_reduce(lnsum[:, :], x1[:, :, :], AX.X, ALU.add))
            step("mean", ts(lnsum[:, :], lnsum[:, :], 1.0 / D, None, ALU.mult))
            step("centred", tt(xc[:, :, :], x1[:, :, :], per_token(lnsum[:, :]), ALU.subtract))
            step("square", tt(sqb[:, :, :], xc[:, :, :], xc[:, :, :], ALU.mult))
            step("sumsq", v.tensor_reduce(lnvar[:, :], sqb[:, :, :], AX.X, ALU.add))
            step("lnvar", ts(lnvar[:, :], lnvar[:, :], 1.0 / D, LN_EPS, ALU.mult, ALU.add))
            set_wait(dve, set_pool, SET_POOL, "lnr")
            step("xln", tt(xc[:, :, :], xc[:, :, :], per_token(lnr[:, :]), ALU.mult))
            dve.wait_ge(set_act, 1)
            step("bot", ts(bot[:, :], bo[:, :], tx[0:S, 0:1], None, ALU.mult))
            set_wait(dve, set_pe, SET_PE, "wqT")
            step("wqT", cp(wqT[:, :, :].rearrange("p (a k) d -> p a (k d)", a=2), psum[:, 0:2, :]))
            set_wait(dve, set_pe, SET_PE, "wkT")
            step("wkT", cp(wkT[:, :, :].rearrange("p (a k) c -> p a (k c)", a=2), psum[:, 2:4, 0:4 * C]))
            set_wait(dve, set_pe, SET_PE, "wvT")
            step("wvT", cp(wvT[:, :, :].rearrange("p (a k) c -> p a (k c)", a=2), psum[:, 4:6, 0:4 * C]))
            for g in range(2):
                set_wait(dve, set_pe, SET_PE, f"xlnT{g}")
                step(f"xlnT{g}", cp(xlnT[:, g * GW:(g + 1) * GW], psum[:, AUXB + g, 0:GW]))
            Mh_r = Mh[:, :, :].rearrange("p (a r) c -> p r a c", r=2)
            Nh_r = Nh[0:C, :, :].rearrange("p (a r) c -> p r a c", r=2)
            set_wait(dve, set_pe, SET_PE, "Mh")
            for r in range(2):
                cp(Mh_r[:, r, 0:4, :], psum[:, 2 * r, 0:4 * C].rearrange("p (k c) -> p k c", c=C))
                step(f"Mh{r}", cp(Mh_r[:, r, 4:8, :],
                                  psum[:, 2 * r + 1, 0:4 * C].rearrange("p (k c) -> p k c", c=C)))
            set_wait(dve, set_pe, SET_PE, "Nh")
            for r in range(2):
                for h in range(2):
                    ins = ts(Nh_r[:, r, 4 * h:4 * h + 4, 0:D],
                             psum[0:C, 4 + 2 * r + h, :].rearrange("p (k c) -> p k c", c=D),
                             tx[0:C, 0:1], None, ALU.mult)
                step(f"Nh{r}", ins)
            for g in range(2, 4):
                set_wait(dve, set_pe, SET_PE, f"xlnT{g}")
                step(f"xlnT{g}", cp(xlnT[:, g * GW:(g + 1) * GW], psum[:, g - 2, 0:GW]))
            step("x1", tt(x1[:, :, :], x1[:, :, :], bot[:, :].unsqueeze(1).broadcast_to([S, B, D]), ALU.add))

            set_wait(dve, set_pool, SET_POOL, "head_mask")

            def f_inc(ins, c, name, wait=False):
                ins.then_inc(f_step, 1)
                if wait:
                    wait_apart(dve, f_step, f_at(c, name))

            def aux(seq, free, par, unit, b, parity, out_of, last):
                kind, n = unit
                bank = psum[:, AUXB + par, :]
                if kind == "ln":
                    wait_apart(dve, aux_free, free)
                    f_inc(v.bn_stats(stats[:, :], x1[:, bat(b), :]), b, "stats", True)
                    f_inc(v.bn_aggr(aggr[:, :], stats[:, :]), b, "aggr", True)
                    return
                if kind == "xf":
                    dve.wait_ge(pool_step, p_at(b, "rr"))
                    f_inc(ts(xf[:, :], x1[:, bat(b), :].squeeze(1), aggr[:, 0:1], pcol("rstd"),
                             ALU.subtract, ALU.mult), b, "xf")
                    f_inc(ts(hn[:, :], x1[:, bat(b), :].squeeze(1), aggr[:, 0:1], pcol("rr"),
                             ALU.subtract, ALU.mult), b, "h", True)
                    return
                if kind == "rs":
                    wait_apart(dve, aux_free, free)
                    f_inc(v.bn_stats(stats2[:, :], x2[:, bat(b), :]), b, "stats2", True)
                    f_inc(v.bn_aggr(aggr2[:, :], stats2[:, :]), b, "aggr2", True)
                    return
                if kind == "h2":
                    dve.wait_ge(pool_step, p_at(b, "r2"))
                    f_inc(ts(hn2[:, :], x2[:, bat(b), :].squeeze(1), pcol("r2"), None, ALU.mult), b, "h2")
                    return
                if kind in ("t", "q"):
                    dve.wait_ge(hi_out, b * 7 + (n + 1 + 3 * (kind == "q")))
                    if kind == "t":
                        cols = slice(512 * n, min(KV, 512 * (n + 1)))
                        hi, lo = cT_hi[parity][0:C, cols], cT_lo[parity][:, cols]
                        w = cols.stop - cols.start
                    else:
                        w = GW
                        hi, lo = (t[parity][0:C, GW * n:GW * (n + 1)] for t in (qk_hi, qk_lo))
                    tt(lo, bank[0:C, 0:w], hi, ALU.subtract).then_inc(aux_free, 1)
                    return
                if by_act(unit):
                    return
                dve.wait_ge(aux_full, seq + 1)
                if kind == "p":
                    rt, part = divmod(n, MP)
                    w = min(MW, KV - part * MW)
                    r = rows_of(rt)
                    v.tensor_reduce(mx[0:r, rt, part:part + 1], bank[0:r, 0:w], AX.X, ALU.max)\
                        .then_inc(aux_free, 1)
                    if n == NPU - 1:
                        dve.wait_ge(aux_free, free + 1)
                        v.tensor_reduce(mx_row[:, :], mx[:, :, :], AX.X, ALU.max).then_inc(max_step, 1)
                        dve.wait_ge(max_step, b * 2 + 1)
                        ts(mneg[:, :], mx_row[:, :], -1.0, SHIFT, ALU.mult, ALU.add).then_inc(max_step, 1)
                elif kind == "m":
                    if not (isinstance(b, int) and b == 0):
                        dve.wait_ge(row_in, b * 32)
                    cp(mrow[:, :], bank[0:RT, 0:P // 2].bitcast(F16)).then_inc(aux_free, 1)
                elif kind in ("y0", "y1"):
                    half = int(kind[1])
                    at = half * Y_STEPS + sum(len(YB[k]) for k in range(n)) + 1
                    nh = len(YB[n])
                    heads = bank[0:S, 0:nh * YW].rearrange("p (k w) -> p k w", w=YW)
                    xb = x1[:, bat(b), :].squeeze(1)
                    dve.wait_ge(aux_free, free)
                    v.reciprocal(y_rc[:, 0:nh], heads[:, :, D]).then_inc(y_step, 1)
                    for k in range(nh):
                        dve.wait_ge(y_step, b * (2 * Y_STEPS) + (at + k))
                        stt(xb, heads[:, k, 0:D], y_rc[:, k:k + 1], xb, ALU.mult, ALU.add)\
                            .then_inc(y_step if k < nh - 1 else aux_free, 1)
                elif n == 0:
                    cp(hT[:, :], bank[:, 0:S]).then_inc(aux_free, 1)
                elif n == 1:
                    f_inc(cp(qT[:, :], bank[:, 0:S]), b, "qT")
                    f_inc(cp(v9[:, :, 0:DS], bank[0:S, 2 * P:3 * P].rearrange("p (h d) -> p h d", d=DS)), b, "v")
                    tt(kbd[:, :, :], bank[:, P:P + S].unsqueeze(1).broadcast_to([P, H, S]),
                       head_mask[:, :].unsqueeze(2).broadcast_to([P, H, S]), ALU.mult).then_inc(aux_free, 1)
                elif n < 6:
                    g = n - 2
                    sc = bank[0:S, 0:GW].rearrange("p (k s) -> p k s", s=S)
                    f_inc(v.tensor_reduce(mx4[:, g, :], sc, AX.X, ALU.max), b, f"mx{g}", True)
                    tt(ex[:, g, :, :], sc, mx4[:, g, :].unsqueeze(2).broadcast_to([S, 4, S]),
                       ALU.subtract).then_inc(aux_free, 1)
                elif n == 10:
                    o9 = bank[0:S, 0:H * (DS + 1)].rearrange("p (h d) -> p h d", d=DS + 1)
                    f_inc(v.reciprocal(s_rc[:, :], o9[:, :, DS]), b, "rc", True)
                    tt(sctx[:, :, :], o9[:, :, 0:DS], s_rc[:, :].unsqueeze(2).broadcast_to([S, H, DS]),
                       ALU.mult).then_inc(aux_free, 1)
                elif n == 11:
                    cp(sctxT[:, :], bank[:, 0:S]).then_inc(aux_free, 1)
                elif n == 12:
                    tt(x2[:, bat(b), :].squeeze(1), bank[0:S, 0:D], xf[:, :], ALU.add).then_inc(aux_free, 1)
                else:
                    cp(h2T[:, tok(b)], bank[:, 0:S]).then_inc(aux_free, 1)

            run_aux(aux, PREP, 0, "prep", 0)

            def body(b, kind, parity):
                for i in range(UNITS):
                    one, two, three = steps(kind)[0][i]
                    run_aux(aux, one, b, kind, parity)
                    if i and i - 1 not in LO_POOL:
                        probs_rest(dve, v, b, i - 1)
                    elif not i and kind != "first":
                        probs_rest(dve, v, b - 1, UNITS - 1)
                    run_aux(aux, two, b, kind, parity)
                    run_aux(aux, three, b, kind, parity)

            batches(dve, body)
            probs_rest(dve, v, B - 1, UNITS - 1)
            run_aux(aux, LAST, B, "end", 0)

            count = [0]

            def link(ins):
                count[0] += 1
                ins.then_inc(top, 1)
                dve.wait_ge(top, count[0])

            def be(t):
                return t.unsqueeze(2).broadcast_to([S, B, E])

            logits = psum[0:S, ACCB + 1, 0:B * E].rearrange("p (b e) -> p b e", e=E)
            dve.wait_ge(logit_full, 1)
            link(v.tensor_reduce(rt_m[:, :], logits, AX.X, ALU.max))
            link(tt(rt_p[:, :, :], logits, be(rt_m[:, :]), ALU.subtract))
            assert count[0] == T_SUB
            dve.wait_ge(silu_out, 1)
            link(v.tensor_reduce(rt_m[:, :], rt_p[:, :, :], AX.X, ALU.add))
            link(v.reciprocal(rt_m[:, :], rt_m[:, :]))
            link(tt(rt_p[:, :, :], rt_p[:, :, :], be(rt_m[:, :]), ALU.mult))
            for e in range(E):
                link(v.memset(rt_no[:, :, e:e + 1], float(E - e)))
            for s, top_p in ((0, rt_a), (1, rt_b)):
                link(v.tensor_reduce(top_p[:, :], rt_p[:, :, :], AX.X, ALU.max))
                link(tt(rt_s[s][:, :, :], rt_p[:, :, :], be(top_p[:, :]), ALU.is_equal))
                link(tt(rt_s[s][:, :, :], rt_s[s][:, :, :], rt_no[:, :, :], ALU.mult))
                link(v.tensor_reduce(rt_m[:, :], rt_s[s][:, :, :], AX.X, ALU.max))
                link(tt(rt_s[s][:, :, :], rt_no[:, :, :], be(rt_m[:, :]), ALU.is_equal))
                if s == 0:
                    link(stt(rt_p[:, :, :], rt_s[0][:, :, :], -2.0, rt_p[:, :, :], ALU.mult, ALU.add))
            link(tt(rt_e[:, :], rt_b[:, :], rt_a[:, :], ALU.subtract))
            assert count[0] == T_D, count[0]
            dve.wait_ge(silu_out, 2)
            link(ts(rt_a[:, :], rt_e[:, :], 1.0, None, ALU.add))
            link(v.reciprocal(rt_a[:, :], rt_a[:, :]))
            link(tt(rt_b[:, :], rt_a[:, :], rt_e[:, :], ALU.mult))
            link(tt(rt_s[0][:, :, :], rt_s[0][:, :, :], be(rt_a[:, :]), ALU.mult))
            link(tt(rt_s[1][:, :, :], rt_s[1][:, :, :], be(rt_b[:, :]), ALU.mult))
            link(tt(comb[:, :, 0:E], rt_s[0][:, :, :], rt_s[1][:, :, :], ALU.add))
            link(v.memset(comb[:, :, E:E + 1], 1.0))

            def hidden_unit(q, n):
                dve.wait_ge(silu_out, q * EU + (n + 3))
                wait_past(dve, down_full, q * EU + max(n - 2, 0))
                tt(hidden[:, n % 3, :], silu[:, n % 3, :], psum[:, 2 * (n % 2) + 1, 0:GW], ALU.mult).then_inc(hid, 1)

            def add_expert(q, e):
                dve.wait_ge(down_full, q * EU + NF * (e + 1))
                if e:
                    dve.wait_ge(sum2, q * 4 * (E + 1) + 4 * e)
                for k in range(4):
                    xb = x2[:, bat(q * 4 + k), :].squeeze(1)
                    w = comb[:, bat(q * 4 + k), e]
                    stt(xb, psum[0:S, AUXB + e % 2, k * D:(k + 1) * D], w, xb, ALU.mult, ALU.add).then_inc(sum2, 1)

            def group(q):
                for n in range(EU):
                    hidden_unit(q, n)
                    if n >= 3 and n % 2 == 1:
                        add_expert(q, (n - 3) // 2)
                add_expert(q, E)
                dve.wait_ge(sum2, (q + 1) * 4 * (E + 1))
                four = cut(q, 4)
                stt(sqb[:, four, :], x2[:, four, :], tf[0:S, 0:1], x1[:, four, :], ALU.mult, ALU.add).then_inc(fin, 1)

            groups(dve, group)


_INS = ["x", "ctx_768", "g_xattn", "g_ffn", "L0_xattn_w_q", "L0_xattn_w_k", "L0_xattn_w_v", "L0_xattn_w_o",
        "L0_xattn_b_o", "L0_ffn_norm1_w", "L0_ffn_norm2_w", "L0_ffn_wq", "L0_ffn_wk", "L0_ffn_wv", "L0_ffn_wo",
        "L0_ffn_router_w", "L0_ffn_sh_gate", "L0_ffn_sh_up", "L0_ffn_sh_down", "L0_ffn_e_gate", "L0_ffn_e_up",
        "L0_ffn_e_down"]
_OUTS = [((16, 100, 128), "float32")]


def kernel(**inputs):
    import numpy as _np
    import concourse.bacc as _bacc
    from concourse import mybir as _mybir
    from concourse.bass_utils import run_bass_kernel_spmd as _run

    nc = _bacc.Bacc("TRN2", target_bir_lowering=False, num_devices=1)
    arrays, args = {}, []
    for name in _INS:
        a = _np.ascontiguousarray(inputs[name])
        arrays[f"in_{name}_dram"] = a
        args.append(nc.dram_tensor(f"in_{name}_dram", a.shape, _mybir.dt.from_np(a.dtype), kind="ExternalInput").ap())
    for i, (shape, dtype) in enumerate(_OUTS):
        dt = _mybir.dt.from_np(_np.dtype(dtype))
        args.append(nc.dram_tensor(f"out_{i}_dram", shape, dt, kind="ExternalOutput").ap())
    flamingo_kernel(nc, *args)
    r = _run(nc, [arrays], core_ids=[0])
    return r.results[0]["out_0_dram"]
```

```python
from contextlib import ExitStack
from math import log

import concourse.bass as bass
from concourse import mybir

F32 = mybir.dt.float32
F16 = mybir.dt.float16
ALU = mybir.AluOpType
ACT = mybir.ActivationFunctionType
AX = mybir.AxisListType

LN_EPS = 1e-5
RMS_EPS = 1e-6
P = 128


def flamingo_kernel(nc, x, ctx, g_xattn, g_ffn, w_q, w_k, w_v, w_o, b_o, norm1_w, norm2_w,
                    wq, wk, wv, wo, router_w, sh_gate, sh_up, sh_down, e_gate, e_up, e_down, out):
    B, S, D = x.shape
    KV, C = ctx.shape[1:]
    DH = 64
    H = w_q.shape[1] // DH
    DS = D // H
    E, _, F = e_gate.shape
    NF = F // P
    FULL = KV // P
    REM = KV - FULL * P
    CH = FULL + 1
    HALF = H // 2
    GW = 4 * S
    ROWS = H * S
    UNITS = 2 * CH
    RT = -(-ROWS // P)
    MW = 512
    MP = -(-KV // MW)
    SHIFT = 10 * log(2.0) * DH ** 0.5
    YB = [(0, 1, 2), (3, 4, 5), (6, 7)]
    YW = D + 1

    EU = (E + 1) * NF

    plan = {i: [] for i in range(UNITS)}
    for n, i in enumerate((0, 0, 1)):
        plan[i].append(("t", n))
    for n, i in enumerate((1, 1, 2, 2)):
        plan[i].append(("q", n))
    for n, i in enumerate((2, 3, 4)):
        plan[i].append(("y1", n))
    for n, i in enumerate((15, 16, 17)):
        plan[i].append(("y0", n))
    plan[6].append(("ln", 0))
    plan[8].append(("xf", 0))
    for n, i in enumerate((8, 9, 10, 11, 12, 13, 12, 13, 14, 15, 16, 18, 19, 23)):
        plan[i].append(("f", n))
    plan[20].append(("rs", 0))
    plan[22].append(("h2", 0))
    CTX_AT = 3
    Y0_AT = 18
    LO_POOL = (6, 8, 10, 12, 14, 16, 18, 20)
    NPU = RT * MP
    F_LOAD = {0: .3, 1: 2.1, 6: 0, 7: 0, 8: 0, 9: 0, 10: .6, 11: .3, 12: .3, 13: .3}
    LOAD = {"t": .7, "q": .6, "y0": 0.55, "y1": 0.55, "ln": .5, "xf": .4, "rs": .5, "h2": .2}
    load = {i: sum(F_LOAD.get(u[1], 1.1) if u[0] == "f" else LOAD[u[0]] for u in plan[i]) for i in plan}
    for i in plan:
        load[i] += 0 if i - 1 in LO_POOL else .9
    share = {i: 0 for i in range(3, 21)}
    for n in range(NPU):
        i = min(share, key=lambda i: (load[i], i))
        share[i] += 1
        load[i] += .6
    n = 0
    for i in share:
        for _ in range(share[i]):
            plan[i].append(("p", n))
            n += 1
    plan[21].append(("m", 0))
    ROUTER = ["max", "sub", "sum", "inv", "prob", "best0", "tie0", "rank0", "first0", "pick0", "drop",
              "best1", "tie1", "rank1", "first1", "pick1", "gap", "norm", "weight0", "weight1",
              "weigh0", "weigh1", "add", "shared"]
    RT_CUTS = [0, 2, 5, 7, 9, 11, 13, 15, 17, 19, 22, 24]
    RT_UNITS = len(RT_CUTS) - 1
    RT_EXPS = {0: "sub", 7: "gap"}
    plan[2].append(("r", 0))
    for n in range(RT_UNITS):
        plan[4 + n].append(("rt", n))
    for n in range(1, 4):
        plan[2 * n - 2].append(("la", n))
        plan[2 * n - 1].append(("lb", n))
        plan[2 * n + 2].append(("lc", n))
        plan[2 * n + 3].append(("x", n))
    for n in range(4):
        plan[10 + n].append(("nh", n))
        plan[13 + n].append(("x1", n))
    PREP = [("t", n) for n in range(3)] + [("q", n) for n in range(4)] + \
           [("p", n) for n in range(NPU)] + [("m", 0)]
    E_AFTER = {"ln": 4, "xf": 0, "f2": 0, "f3": 0, "f4": 0, "f5": 0, "f10": 2, "rs": 2, "h2": 0, "r": EU + 4}
    LAST = []
    for unit in [("y1", 0), ("y1", 1), ("y1", 2), ("ln", 0), ("xf", 0)] + [("f", n) for n in range(13)] + \
                [("rs", 0), ("h2", 0), ("f", 13), ("r", 1)]:
        LAST.append(unit)
        name = f"f{unit[1]}" if unit[0] == "f" else unit[0]
        for _ in range(E_AFTER.get(name, 1)):
            m = sum(u[0] == "e" for u in LAST)
            if m < EU + 4:
                LAST.append(("e", m))
    NO_BANK = ("ln", "xf", "rs", "h2", "rt", "e", "la", "lb", "lc", "x1")
    PREPARE = ("y0", "t", "q", "p", "m")
    KINDS_FIRST = PREPARE + ("la", "lb", "lc", "x", "nh", "x1")
    KINDS_MID = PREPARE + ("y1", "f", "ln", "xf", "rs", "h2")
    KINDS_LAST = ("y0", "y1", "f", "r", "ln", "xf", "rs", "h2", "rt")
    flat = [u for i in range(UNITS) for u in plan[i] if u[0] not in NO_BANK]
    A = sum(u[0] in KINDS_MID for u in flat)
    A_FIRST = sum(u[0] in KINDS_FIRST for u in flat)
    A_LAST = sum(u[0] in KINDS_LAST for u in flat)
    AT_FIRST = len(PREP)
    AT_LOOP = AT_FIRST + A_FIRST

    END = AT_LOOP + A * (B - 2) + A_LAST

    def by_act(u):
        return u[0] == "f" and 6 <= u[1] < 10

    def numbered(units):
        k, free, at = 0, 0, {}
        for u in units:
            at[u] = k, free
            k += u[0] not in NO_BANK
            free += u[0] not in NO_BANK and not by_act(u)
        return at

    def steps(kind):
        kinds = {"first": KINDS_FIRST, "last": KINDS_LAST}.get(kind, KINDS_MID)
        by_place = [[u for u in plan[i] if u[0] in kinds] for i in range(UNITS)]
        at = numbered([u for us in by_place for u in us])
        thirds = [[us[len(us) * k // 3:len(us) * (k + 1) // 3] for k in range(3)] for us in by_place]
        return thirds, at

    def aux_base(b, kind):
        fixed = {"prep": (0, 0), "first": (AT_FIRST, AT_FIRST), "end": (END, END - 4 * (B - 2) - 4)}
        return fixed.get(kind) or ((b - 1) * A + AT_LOOP, (b - 1) * (A - 4) + AT_LOOP)

    ODD = {"prep": 0, "first": AT_FIRST % 2, "odd": AT_LOOP % 2, "even": (AT_LOOP + A) % 2,
           "last": (AT_LOOP + A * (B - 2)) % 2, "end": END % 2}

    def batch_of(unit, b):
        return b + {"t": 1, "q": 1, "p": 1, "m": 1, "y0": 0}.get(unit[0], -1)

    F_STEPS = ["stats", "aggr", "xf", "h", "qT", "v", "mx0", "mx1", "mx2", "mx3", "rc",
               "stats2", "aggr2", "h2"]
    NFS = len(F_STEPS)
    P_STEPS = ["var+eps", "rstd", "rstd2", "ms", "ms+eps", "r", "rr", "mean2", "ms2", "ms2+eps", "r2"]
    NPS = len(P_STEPS)
    SET_POOL = ["-1/2", "zero ident", "ident", "zero ident16", "ident16", "lnr0", "Nh right", "Nh below",
                "Nh corner", "ones cT0", "pad c_hi0", "ones c_hi0", "pad c_lo0", "ones cT1", "pad c_hi1",
                "ones c_hi1", "pad c_lo1", "mx", "ones v9", "ones mask", "mask above", "head_mask",
                "n1"] + [f"rank of {e}" for e in range(E)] + ["rw", "lnr1", "lnr2", "lnr3"]
    LN_A, LN_B = ["sum", "mean", "centred"], ["square", "sumsq", "lnvar"]
    SET_DVE = [f"{n}0" for n in LN_A + LN_B] + ["wqT", "xln0", "bot", "xlnT0", "Mh0"] + \
              [f"{n}{g}" for g, ns in ((1, LN_A), (1, LN_B), (2, LN_A), (2, LN_B), (1, ["xln"]), (3, LN_A), (3, LN_B),
                                       (2, ["xln"]), (3, ["xln"])) for n in ns] + [f"x1 {g}" for g in range(4)]
    SET_ACT = ["tx", "tf", "wkT", "wvT", "Mh1"]
    SET_PE = ["wqT", "wkT", "wvT", "xlnT0", "Mh"]
    Y_READ = [2, 5, 7, 10, 13, 15]
    LAG = 3
    HS = 6
    NW_PARTS = 6

    with ExitStack() as stack:
        def sb(name, shape, dt=F32):
            return stack.enter_context(nc.sbuf_tensor(name, shape, dt))

        def sem(name):
            return stack.enter_context(nc.semaphore(name))

        ident = sb("ident", [P, P])
        ident16 = sb("ident16", [P, P], F16)
        head_mask = sb("head_mask", [P, H])
        minus_half = sb("minus_half", [P, H])
        x1 = sb("x1", [S, B, D])
        x2 = sb("x2", [S, B, D])
        xlnT = sb("xlnT", [D, B * S])
        h2T = sb("h2T", [D, B * S])
        Mh = sb("Mh", [D, H, C])
        Nh = sb("Nh", [C + 1, H, YW])
        ctx_nat = sb("ctx_nat", [P, CH, C])
        c_hi = [sb(f"c_hi{q}", [P, CH, P], F16) for q in range(2)]
        c_lo = [sb(f"c_lo{q}", [P, CH, P], F16) for q in range(2)]
        cT_hi = [sb(f"cT_hi{q}", [C + 1, KV], F16) for q in range(2)]
        cT_lo = [sb(f"cT_lo{q}", [C, KV], F16) for q in range(2)]
        qk_hi = [sb(f"qk_hi{q}", [C + 1, ROWS], F16) for q in range(2)]
        qk_lo = [sb(f"qk_lo{q}", [C, ROWS], F16) for q in range(2)]
        p32 = sb("p32", [P, 3, 2, GW])
        p_hi = sb("p_hi", [P, 3, 2, GW], F16)
        p_lo = sb("p_lo", [P, 3, 2, GW], F16)
        acc_sb = [sb(f"acc_sb{g}", [C + 1, 2, GW]) for g in range(2)]
        mx = sb("mx", [P, RT, MP])
        mx_row = sb("mx_row", [P, RT])
        mneg = sb("mneg", [P, RT], F16)
        mrow = sb("mrow", [RT, P], F16)
        y_rc = sb("y_rc", [S, 3])
        y_sum = sb("y_sum", [S, D])
        y_sb = sb("y_sb", [S, 2, 3, D])
        n1 = sb("n1", [D, 1])
        n2 = sb("n2", [D, 1])
        sw = sb("sw", [D, 4, D])
        stats = sb("stats", [S, 6])
        aggr = sb("aggr", [S, 2])
        stats2 = sb("stats2", [S, 6])
        aggr2 = sb("aggr2", [S, 2])
        ps = sb("ps", [S, NPS])
        xf = sb("xf", [S, D])
        hn = sb("hn", [S, D])
        hT = sb("hT", [D, S])
        qT = sb("qT", [D, S])
        kbd = sb("kbd", [D, H, S])
        v9 = sb("v9", [S, H, DS + 1])
        mx4 = sb("mx4", [S, 4, 4])
        ex = sb("ex", [S, 4, 4, S])
        pT = sb("pT", [S, 4, GW])
        s_rc = sb("s_rc", [S, H])
        sctx = sb("sctx", [S, H, DS])
        sctxT = sb("sctxT", [D, S])
        hn2 = sb("hn2", [S, D])
        wg = sb("wg", [D, E + 1, F])
        wu = sb("wu", [D, E + 1, F])
        wd = sb("wd", [P, E + 1, NF, D])
        w_hi = [sb(f"{w}_hi", [P, E + 1, F], F16) for w in ("wg", "wu", "wd")]
        w_lo = [sb(f"{w}_lo", [P, E + 1, F], F16) for w in ("wg", "wu", "wd")]
        h_hi = sb("h_hi", [D, B * S], F16)
        h_lo = sb("h_lo", [D, B * S], F16)
        rw = sb("rw", [D, E])
        gx = sb("gx", [P, 1])
        gf = sb("gf", [P, 1])
        tx = sb("tx", [P, 1])
        tf = sb("tf", [P, 1])
        bo = sb("bo", [S, D])

        psum = stack.enter_context(nc.psum_tensor("psum", [P, 8, 512], F32))
        ACCB, AUXB = 4, 6

        wqk_in, x_in, w_in, e_in = sem("wqk_in"), sem("x_in"), sem("w_in"), sem("e_in")
        set_pool, set_dve, set_act, set_pe = sem("set_pool"), sem("set_dve"), sem("set_act"), sem("set_pe")
        w_split = sem("w_split")
        ctx_in, row_in = sem("ctx_in"), sem("row_in")
        ctx_hi, split = sem("ctx_hi"), sem("split")
        scores, probs_hi = sem("scores"), sem("probs_hi")
        probs_lo, lo_pool = sem("probs_lo"), sem("lo_pool")
        pv, acc_out = sem("pv"), sem("acc_out")
        aux_full, aux_free, hi_out, pt_out = sem("aux_full"), sem("aux_free"), sem("hi_out"), sem("pt_out")
        max_step = sem("max_step")
        y_rcp, y_add = sem("y_rcp"), sem("y_add")
        f_step, pool_step, exp_out = sem("f_step"), sem("pool_step"), sem("exp_out")
        top, router_exp = sem("top"), sem("router_exp")
        h_hi_out, h_lo_out = sem("h_hi_out"), sem("h_lo_out")
        gu_full, silu_out, hid = sem("gu_full"), sem("silu_out"), sem("hid")
        hid_hi_out, hid_lo_out = sem("hid_hi_out"), sem("hid_lo_out")
        down_full, sum2 = sem("down_full"), sem("sum2")
        fin, out_done = sem("fin"), sem("out_done")

        def f_at(c, name):
            return c * NFS + (F_STEPS.index(name) + 1)

        def p_at(c, name):
            return c * NPS + (P_STEPS.index(name) + 1)

        def pcol(name):
            k = P_STEPS.index(name)
            return ps[:, k:k + 1]

        def lo_made(b, i):
            if i < 0:
                return lo_made(b - 1, i + UNITS)
            by_pool = sum(u < i for u in LO_POOL)
            if i in LO_POOL:
                return lo_pool, b * len(LO_POOL) + (by_pool + 1)
            return probs_lo, b * (UNITS - len(LO_POOL)) + (i - by_pool + 1)

        def set_wait(eng, signal, order, name):
            eng.wait_ge(signal, order.index(name) + 1)

        def wait_apart(eng, signal, value):
            if not isinstance(value, int):
                value = eng.to_reg(value)
                eng.wait_ge(w_in, 16)
            eng.wait_ge(signal, value)

        def batches(eng, body):
            body(0, "first", 0)
            with eng.Fori(0, (B - 2) // 2) as r:
                body(r * 2 + 1, "odd", 1)
                body(r * 2 + 2, "even", 0)
            body(B - 1, "last", 1)

        def groups(eng, body, between=lambda: None):
            body(1)
            between()
            with eng.Fori(2, B // 4) as q:
                body(q)

        def wait_past(eng, signal, value):
            if not (isinstance(value, int) and value == 0):
                eng.wait_ge(signal, value)

        def run_aux(aux, units, b, kind, parity):
            at = {"prep": numbered(PREP), "end": numbered(LAST)}.get(kind) or steps(kind)[1]
            base = aux_base(b, kind)
            order = [u for u in at if u[0] not in NO_BANK]
            for u in units:
                on = 0 if kind == "prep" else batch_of(u, b)
                near = 0 if kind == "prep" else batch_of(u, 0)
                k, free = at[u]
                last = order[k - 2] if k >= 2 else None
                last_free = at[last][1] + 1 if last else k - 1
                aux(base[0] + k, base[1] + free, (ODD[kind] + k) % 2, u, on, (parity + near) % 2,
                    lambda other: base[1] + at[other][1] + 1,
                    (pt_out, batch_of(last, b) * 4 + (last[1] - 5)) if last and by_act(last)
                    else (aux_free, base[1] + last_free))

        def cut(q, n):
            return slice(q * n, q * n + n) if isinstance(q, int) else bass.ds(q * n, n)

        def tok(b):
            return slice(b * S, b * S + S) if isinstance(b, int) else bass.ds(b * S, S)

        def bat(b, n=1):
            return slice(b, b + n) if isinstance(b, int) else bass.ds(b, n)

        def kc(j):
            m = P if j < FULL else REM
            return slice(j * P, j * P + m), m

        def part_cols(part):
            return slice(PARTS[part][0] * S, PARTS[part][1] * S)

        def rows_of(t):
            return min(P, ROWS - t * P)

        CTX_PARTS = ((P, slice(0, FULL)), (REM, slice(FULL, CH)))
        WQK_LOADS, X_LOADS, W_LOADS, E_LOADS = 2, 6, 6, 2 * 2 + E + 1 + 2
        PARTS = ((0, B - 4), (B - 4, B))

        wq_nat = p32[:, :, :, :].rearrange("p a k w -> p (a k w)")[:, 0:H * DH]

        def as_f32(t, rows, width):
            return t[:, :, :].rearrange("p e f -> p (e f)").bitcast(F32)[0:rows, 0:width]

        wk_nat = as_f32(w_hi[0], C, H * DH)
        wv_nat = as_f32(w_hi[1], C, H * DH)
        wo_nat = as_f32(w_hi[2], P, H // 2 * D).rearrange("p (a d) -> p a d", d=D)
        wqT = as_f32(w_lo[0], P, H // 2 * D).rearrange("p (a d) -> p a d", d=D)
        wkT = as_f32(w_lo[1], P, H // 2 * C).rearrange("p (a c) -> p a c", c=C)
        wvT = as_f32(w_lo[2], P, H // 2 * C).rearrange("p (a c) -> p a c", c=C)
        xc = x2
        lnsum = sb("lnsum", [S, B])
        lnvar = sb("lnvar", [S, B])
        lnr = sb("lnr", [S, B])
        bot = sb("bot", [S, D])
        sqb = sb("sqb", [S, B, D])
        rt_m = sb("rt_m", [S, B])
        rt_a = sb("rt_a", [S, B])
        rt_b = sb("rt_b", [S, B])
        rt_e = sb("rt_e", [S, B])
        rt_no = sb("rt_no", [S, E])
        rt_p, rt_s0, rt_s1 = (xlnT[0:S, k * B * E:(k + 1) * B * E].rearrange("p (b e) -> p b e", e=E)
                              for k in range(3))
        rt_s = (rt_s0, rt_s1)
        comb = xlnT[0:S, 3 * B * E:3 * B * E + B * (E + 1)].rearrange("p (b e) -> p b e", e=E + 1)
        silu = p32[:, :, 0, :]
        hidden = p32[:, :, 1, :]
        hid_hi = p_hi[:, :, :, :].rearrange("p a k w -> p (a k) w")
        hid_lo = p_lo[:, :, :, :].rearrange("p a k w -> p (a k) w")

        def probs_rest(eng, engine, b, i):
            m = kc(i % CH)[1]
            eng.wait_ge(probs_hi, b * UNITS + (i + 1))
            if not (isinstance(b, int) and b == 0 and i < 3):
                eng.wait_ge(pv, b * UNITS + (i - 2))
            engine.tensor_tensor(p_lo[0:m, i % 3, :, :], p32[0:m, i % 3, :, :], p_hi[0:m, i % 3, :, :],
                                 ALU.subtract).then_inc(lo_made(b, i)[0], 1)

        Mh_r = Mh[:, :, :].rearrange("p (a r) c -> p r a c", r=2)
        Nh_r = Nh[0:C, :, :].rearrange("p (a r) c -> p r a c", r=2)
        wd_flat = wd[:, :, :, :].rearrange("p e a d -> p e (a d)")

        block = stack.enter_context(nc.Block())

        @block.sync
        def _(sp):
            def load(dst, src, signal=w_in):
                sp.dma_start(dst, src).then_inc(signal, 16)

            def load_ctx(b):
                sp.dma_start(ctx_nat[:, 0:FULL, :], ctx[bat(b), 0:FULL * P, :].rearrange(
                    "b (p j) c -> p (b j) c", j=FULL)).then_inc(ctx_in, 16)
                sp.dma_start(ctx_nat[0:REM, FULL, :], ctx[bat(b), FULL * P:KV, :].rearrange(
                    "b r c -> (b r) c")).then_inc(ctx_in, 16)

            def send_row(b, parity, free):
                sp.wait_ge(aux_free, free + 1)
                sp.dma_start(qk_hi[parity][C:C + 1, 0:(RT - 1) * P], mrow[0:RT - 1, :]).then_inc(row_in, 16)
                sp.dma_start(qk_hi[parity][C:C + 1, (RT - 1) * P:ROWS],
                             mrow[RT - 1:RT, 0:rows_of(RT - 1)]).then_inc(row_in, 16)

            load(wq_nat, w_q, wqk_in)
            load(wk_nat[:, :], w_k, wqk_in)
            load(x1[:, 0:4, :], x[0:4].rearrange("b s d -> s b d"), x_in)
            load(wv_nat[:, :], w_v, x_in)
            load(gx[:, :], g_xattn.partition_broadcast(P), x_in)
            load(gf[:, :], g_ffn.partition_broadcast(P), x_in)
            load(bo[:, :], b_o.partition_broadcast(S), x_in)
            load_ctx(0)
            load(wo_nat[:, :, :], w_o.rearrange("(a k) d -> k a d", k=P), x_in)
            load(x1[:, 4:B, :], x[4:B].rearrange("b s d -> s b d"))
            load(n1[:, :], norm1_w.rearrange("(p a) -> p a", a=1))
            for k, w in enumerate((wq, wk, wv, wo)):
                load(sw[:, k, :], w)
            load(n2[:, :], norm2_w.rearrange("(p a) -> p a", a=1), e_in)
            load(rw[:, :], router_w, e_in)
            for dst, many, one in ((wg, e_gate, sh_gate), (wu, e_up, sh_up)):
                load(dst[:, 0:E, :], many.rearrange("e d f -> d e f"), e_in)
                load(dst[:, E, :], one, e_in)
            for e in range(E):
                load(wd[:, e, :, :], e_down[e].rearrange("(a p) d -> p a d", p=P), e_in)
            load(wd[:, E, :, :], sh_down.rearrange("(a p) d -> p a d", p=P), e_in)

            def load_after(b):
                sp.wait_ge(hi_out, b * 7 + 3)
                sp.wait_ge(split, (b + 1) * len(CTX_PARTS))
                load_ctx(b + 1)

            def row_of(b, kind, parity):
                if kind != "first":
                    sp.wait_ge(scores, b * UNITS)
                send_row(b + 1, 1 - parity, aux_base(b, kind)[1] + steps(kind)[1][("m", 0)][1])

            load_after(0)
            send_row(0, 0, len(PREP) - 1)
            load_after(1)
            row_of(0, "first", 0)
            with sp.Fori(0, (B - 4) // 2) as r:
                for b, kind, parity in ((r * 2 + 1, "odd", 1), (r * 2 + 2, "even", 0)):
                    load_after(b + 1)
                    row_of(b, kind, parity)
            load_after(B - 2)
            row_of(B - 3, "odd", 1)
            row_of(B - 2, "even", 0)
            for q in range(4):
                sp.wait_ge(fin, q + 1)
                sp.dma_start(out[4 * q:4 * q + 4].rearrange("b s d -> s b d"),
                             sqb[:, 4 * q:4 * q + 4, :]).then_inc(out_done, 16)
            sp.wait_ge(out_done, 64)

        @block.gpsimd
        def _(pool):
            g = nc.gpsimd

            def step(name, ins):
                ins.then_inc(set_pool, 1)
                set_wait(pool, set_pool, SET_POOL, name)

            def select(t, base, pattern, cm, op, fill):
                return g.affine_select(out=t[:, :], in_=t[:, :], compare_op=op, fill=fill, base=base,
                                       pattern=pattern, channel_multiplier=cm)

            step("-1/2", g.memset(minus_half[:, :], -0.5))
            step("zero ident", g.memset(ident[:, :], 0.0))
            step("ident", select(ident, 0, [[-1, P]], 1, ALU.not_equal, 1.0))
            step("zero ident16", g.memset(ident16[:, :], 0.0))
            step("ident16", select(ident16, 0, [[-1, P]], 1, ALU.not_equal, 1.0))

            def token_rstd(n):
                set_wait(pool, set_dve, SET_DVE, f"lnvar{n}")
                step(f"lnr{n}", g.tensor_tensor(lnr[:, cut(n, 4)], lnvar[:, cut(n, 4)], minus_half[0:S, 0:4], ALU.pow))

            token_rstd(0)
            step("Nh right", g.memset(Nh[:, :, D:YW], 0.0))
            step("Nh below", g.memset(Nh[C:C + 1, :, 0:D], 0.0))
            step("Nh corner", g.memset(Nh[C:C + 1, :, D:YW], 1.0))
            for q in range(2):
                step(f"ones cT{q}", g.memset(cT_hi[q][C:C + 1, :], 1.0))
                step(f"pad c_hi{q}", g.memset(c_hi[q][:, :, C:P], 0.0))
                step(f"ones c_hi{q}", g.memset(c_hi[q][:, :, C:C + 1], 1.0))
                step(f"pad c_lo{q}", g.memset(c_lo[q][:, :, C:P], 0.0))
            step("mx", g.memset(mx[:, :, :], 0.0))
            step("ones v9", g.memset(v9[:, :, DS:DS + 1], 1.0))
            step("ones mask", g.memset(head_mask[:, :], 1.0))
            step("mask above", select(head_mask, 0, [[-DS, H]], 1, ALU.is_ge, 0.0))
            step("head_mask", select(head_mask, DS - 1, [[DS, H]], -1, ALU.is_ge, 0.0))

            def ctx_lo(b, parity):
                pool.wait_ge(ctx_hi, b + 1)
                for r, js in CTX_PARTS:
                    g.tensor_tensor(c_lo[parity][0:r, js, 0:C], ctx_nat[0:r, js, :],
                                    c_hi[parity][0:r, js, 0:C], ALU.subtract).then_inc(split, 1)

            def add_heads(b, half, n, free_of):
                done = b * 2 * HALF + half * HALF

                def add(n, to, x, y):
                    if n:
                        wait_apart(pool, y_add, done + n)
                    g.tensor_tensor(to, x, y, ALU.add).then_inc(y_add, 1)

                y = y_sb[:, (half * len(YB) + n) % 2, :, :]
                pool.wait_ge(aux_free, free_of((f"y{half}", n)))
                for k, h in enumerate(YB[n]):
                    if h:
                        add(h - 1, y_sum[:, :], y[:, 0, :] if h == 1 else y_sum[:, :], y[:, k, :])
                if n == len(YB) - 1:
                    xb = x1[:, bat(b), :].squeeze(1)
                    add(HALF - 1, xb, xb, y_sum[:, :])

            def small(c, name, ins):
                ins.then_inc(pool_step, 1)
                wait_apart(pool, pool_step, p_at(c, name))

            half = minus_half[0:S, 0:1]

            def norm_1(c):
                var = aggr[:, 1:2]
                wait_apart(pool, f_step, f_at(c, "aggr"))
                small(c, "var+eps", g.tensor_scalar(pcol("var+eps"), var, LN_EPS, None, ALU.add))
                small(c, "rstd", g.tensor_tensor(pcol("rstd"), pcol("var+eps"), half, ALU.pow))
                small(c, "rstd2", g.tensor_tensor(pcol("rstd2"), pcol("rstd"), pcol("rstd"), ALU.mult))
                small(c, "ms", g.tensor_tensor(pcol("ms"), pcol("rstd2"), var, ALU.mult))
                small(c, "ms+eps", g.tensor_scalar(pcol("ms+eps"), pcol("ms"), RMS_EPS, None, ALU.add))
                small(c, "r", g.tensor_tensor(pcol("r"), pcol("ms+eps"), half, ALU.pow))
                small(c, "rr", g.tensor_tensor(pcol("rr"), pcol("r"), pcol("rstd"), ALU.mult))

            def norm_2(c):
                pool.wait_ge(f_step, f_at(c, "aggr2"))
                small(c, "mean2", g.tensor_tensor(pcol("mean2"), aggr2[:, 0:1], aggr2[:, 0:1], ALU.mult))
                small(c, "ms2", g.tensor_tensor(pcol("ms2"), pcol("mean2"), aggr2[:, 1:2], ALU.add))
                small(c, "ms2+eps", g.tensor_scalar(pcol("ms2+eps"), pcol("ms2"), RMS_EPS, None, ALU.add))
                small(c, "r2", g.tensor_tensor(pcol("r2"), pcol("ms2+eps"), half, ALU.pow))

            ctx_lo(0, 0)
            pool.wait_ge(w_in, 16 * W_LOADS)
            step("n1", g.tensor_scalar(sw[:, 0:3, :], sw[:, 0:3, :], n1[:, 0:1], None, ALU.mult))
            for e in range(E):
                step(f"rank of {e}", g.memset(rt_no[:, e:e + 1], float(E - e)))
            pool.wait_ge(e_in, 16 * E_LOADS)
            step("rw", g.tensor_scalar(rw[:, :], rw[:, :], n2[:, 0:1], None, ALU.mult))

            def inputs_lo(part):
                cols = part_cols(part)
                pool.wait_ge(h_hi_out, part + 1)
                g.tensor_tensor(h_lo[:, cols], h2T[:, cols], h_hi[:, cols], ALU.subtract).then_inc(h_lo_out, 1)

            def hidden_lo(q, n):
                pool.wait_ge(hid_hi_out, q * EU + (n + 1))
                g.tensor_tensor(hid_lo[:, n % HS, :], hidden[:, n % 3, :], hid_hi[:, n % HS, :],
                                ALU.subtract).then_inc(hid_lo_out, 1)

            def body(b, kind, parity):
                if kind == "first":
                    token_rstd(1)
                if kind != "last":
                    ctx_lo(b + 1, 1 - parity)
                if kind == "first":
                    token_rstd(2)
                    token_rstd(3)
                at = steps(kind)[1]
                base = aux_base(b, kind)[1]

                def free_of(unit):
                    return base + at[unit][1] + 1

                if kind != "first":
                    for n in range(len(YB)):
                        add_heads(b - 1, 1, n, free_of)
                    norm_1(b - 1)
                for i in range(UNITS):
                    if i == Y0_AT:
                        if kind == "first":
                            set_wait(pool, set_dve, SET_DVE, "x1 3")
                        for n in range(len(YB)):
                            add_heads(b, 0, n, free_of)
                    if i == 9 and kind == "last":
                        inputs_lo(0)
                    if i in LO_POOL:
                        probs_rest(pool, g, b, i)
                if kind != "first":
                    norm_2(b - 1)

            batches(pool, body)

            def free_at_end(unit):
                return aux_base(B, "end")[1] + numbered(LAST)[unit][1] + 1

            for kind, n in LAST:
                if kind == "y1":
                    add_heads(B - 1, 1, n, free_at_end)
                elif kind == "ln":
                    norm_1(B - 1)
                elif kind == "rs":
                    norm_2(B - 1)
                elif kind == "e" and 0 <= n - 2 < EU:
                    hidden_lo(0, n - 2)
            inputs_lo(1)

            def group(q):
                for n in range(EU):
                    hidden_lo(q, n)

            groups(pool, group)

        @block.tensor
        def _(pe):
            mm = nc.tensor.matmul
            tr = nc.tensor.transpose

            pe.wait_ge(wqk_in, 16 * WQK_LOADS)
            set_wait(pe, set_pool, SET_POOL, "ident16")
            for a in range(H // 2):
                t = tr(psum[:, a // 4, (a % 4) * D:(a % 4) * D + D], wq_nat[:, a * P:(a + 1) * P], ident[:, :])
            t.then_inc(set_pe, 1)
            for k, w in enumerate((wk_nat, wv_nat)):
                if w is wv_nat:
                    pe.wait_ge(x_in, 16 * X_LOADS)
                for a in range(H // 2):
                    t = tr(psum[:, 2 + 2 * k + a // 4, (a % 4) * C:(a % 4) * C + C],
                           w[:, a * P:(a + 1) * P], ident[0:C, 0:C])
                t.then_inc(set_pe, 1)
            set_wait(pe, set_dve, SET_DVE, "xln0")
            for k in range(4):
                t = tr(psum[:, AUXB, k * S:(k + 1) * S], xc[:, k, :], ident[0:S, 0:S])
            t.then_inc(set_pe, 1)
            set_wait(pe, set_dve, SET_DVE, "wqT")
            set_wait(pe, set_act, SET_ACT, "wkT")
            for r in range(2):
                for a in range(H // 2):
                    rs = slice(DH * r, DH * r + DH)
                    t = mm(psum[:, 2 * r + a // 4, (a % 4) * C:(a % 4) * C + C], wqT[rs, a, :], wkT[rs, a, :],
                           start=True, stop=True)
            t.then_inc(set_pe, 1)
            set_wait(pe, set_dve, SET_DVE, "Mh0")
            set_wait(pe, set_act, SET_ACT, "Mh1")
            set_wait(pe, set_pool, SET_POOL, "head_mask")

            def score_unit(b, parity, i):
                g, j = divmod(i, CH)
                cols, m = kc(j)
                if isinstance(b, int) and b == 0 and i < 2:
                    pass
                else:
                    pe.wait_ge(probs_hi, b * UNITS + (i - 1))
                if i == 0:
                    pe.wait_ge(row_in, (b + 1) * 32)
                s = i % 2
                outs = [psum[0:m, 2 * s + k, 0:GW] for k in range(2)]
                qs = [slice((2 * g + k) * GW, (2 * g + k + 1) * GW) for k in range(2)]
                for k in range(2):
                    mm(outs[k], cT_hi[parity][:, cols], qk_hi[parity][:, qs[k]], start=True, stop=False)
                for k in range(2):
                    mm(outs[k], cT_hi[parity][0:C, cols], qk_lo[parity][:, qs[k]], start=False, stop=False)
                for k in range(2):
                    t = mm(outs[k], cT_lo[parity][:, cols], qk_hi[parity][0:C, qs[k]], start=False, stop=True)
                t.then_inc(scores, 1)

            def pv_unit(b, parity, i, between=lambda: None):
                j = i % CH
                m = kc(j)[1]
                pe.wait_ge(*lo_made(b, i))
                if i == 0:
                    pe.wait_ge(split, (b + 1) * len(CTX_PARTS))
                if j == 0 and not (isinstance(b, int) and b == 0 and i == 0):
                    pe.wait_ge(acc_out, b * 2 + i // CH)
                outs = [psum[:, ACCB + k, 0:GW] for k in range(2)]
                for w, p in ((c_hi, p_hi), (c_hi, p_lo), (c_lo, p_hi)):
                    for k in range(2):
                        t = mm(outs[k], w[parity][0:m, j, :], p[0:m, i % 3, k, :],
                               start=(j == 0 and w is c_hi and p is p_hi), stop=(j == CH - 1 and w is c_lo))
                    if w is c_hi and p is p_hi:
                        between()
                t.then_inc(pv, 1)

            def gate_up(q, n):
                e, f = divmod(n, NF)
                wait_past(pe, hid, q * EU + max(n - 1, 0))
                fs = slice(f * P, (f + 1) * P)
                for k in range(2):
                    for w, h in ((w_hi, h_hi), (w_hi, h_lo), (w_lo, h_hi)):
                        t = mm(psum[:, 2 * (n % 2) + k, 0:GW], w[k][:, e, fs], h[:, cut(q, GW)],
                               start=(w is w_hi and h is h_hi), stop=(w is w_lo))
                t.then_inc(gu_full, 1)

            def down(q, n):
                e, f = divmod(n, NF)
                pe.wait_ge(hid_lo_out, q * EU + (n + 1))
                if f == 0 and e >= 2:
                    pe.wait_ge(sum2, q * 4 * (E + 1) + 4 * (e - 1))
                elif f == 0:
                    wait_past(pe, sum2, q * 4 * (E + 1))
                for k in range(4):
                    for h, w in ((hid_hi, w_hi), (hid_hi, w_lo), (hid_lo, w_hi)):
                        t = mm(psum[0:S, ACCB + e % 2, k * D:(k + 1) * D], h[:, n % HS, k * S:(k + 1) * S],
                               w[2][:, e, f * D:(f + 1) * D], start=(f == 0 and k == 0 and h is hid_hi and w is w_hi),
                               stop=(f == NF - 1 and k == 3 and h is hid_lo), skip_group_check=True)
                t.then_inc(down_full, 1)

            def aux(seq, free, par, unit, b, parity, out_of, last):
                kind, n = unit
                if kind == "e":
                    if n == 0:
                        pe.wait_ge(w_split, 3 * NW_PARTS)
                        pe.wait_ge(h_lo_out, 1)
                        pe.wait_ge(probs_hi, B * UNITS)
                    if n < EU:
                        gate_up(0, n)
                    if n == LAG:
                        pe.wait_ge(acc_out, B * 2)
                    if 0 <= n - LAG < EU:
                        down(0, n - LAG)
                if kind in NO_BANK:
                    return
                if not (isinstance(seq, int) and seq < 2):
                    pe.wait_ge(*last)
                bank = psum[:, AUXB + par, :]
                if kind == "t":
                    if n == 0:
                        pe.wait_ge(ctx_in, (b + 1) * 32)
                    for k in range(4):
                        m = kc(4 * n + k)[1]
                        t = tr(bank[0:C, k * P:k * P + m], ctx_nat[0:m, 4 * n + k, :], ident[0:m, 0:m])
                elif kind == "q":
                    for k in range(4):
                        t = mm(bank[0:C, k * S:(k + 1) * S], Mh[:, 4 * n + k, :], xlnT[:, tok(b)],
                               start=True, stop=True)
                elif kind == "p":
                    rt, part = divmod(n, MP)
                    if n == 0:
                        pe.wait_ge(aux_free, free)
                    r = rows_of(rt)
                    w = min(MW, KV - part * MW)
                    t = mm(bank[0:r, 0:w], qk_hi[parity][0:C, rt * P:rt * P + r],
                           cT_hi[parity][0:C, part * MW:part * MW + w], start=True, stop=True)
                elif kind == "m":
                    pe.wait_ge(max_step, (b + 1) * 2)
                    t = tr(bank[0:RT, 0:P // 2].bitcast(F16), mneg[:, :], ident16[:, :])
                elif kind == "x":
                    set_wait(pe, set_dve, SET_DVE, f"xln{n}")
                    for k in range(4):
                        t = tr(bank[:, k * S:(k + 1) * S], xc[:, 4 * n + k, :], ident[0:S, 0:S])
                elif kind == "nh":
                    r, a0 = n // 2, 4 * (n % 2)
                    for a in range(a0, a0 + 4):
                        rs = slice(DH * r, DH * r + DH)
                        t = mm(bank[0:C, (a - a0) * D:(a - a0 + 1) * D], wvT[rs, a, :], wo_nat[rs, a, :],
                               start=True, stop=True)
                elif kind == "r":
                    if n == 0:
                        set_wait(pe, set_pool, SET_POOL, "rw")
                    pe.wait_ge(aux_free, free)
                    for k in range(*PARTS[n]):
                        t = mm(bank[0:S, k * E:(k + 1) * E], h2T[:, tok(k)], rw[:, :], start=True, stop=True)
                elif kind in ("y0", "y1"):
                    half = int(kind[1])
                    if n == 0:
                        pe.wait_ge(acc_out, b * 2 + (half + 1))
                    for k, h in enumerate(YB[n]):
                        t = mm(bank[0:S, k * YW:(k + 1) * YW], acc_sb[half][:, h // 4, (h % 4) * S:(h % 4 + 1) * S],
                               Nh[:, half * HALF + h, :], start=True, stop=True)
                elif n == 0:
                    pe.wait_ge(f_step, f_at(b, "h"))
                    t = tr(bank[:, 0:S], hn[:, :], ident[0:S, 0:S])
                elif n == 1:
                    pe.wait_ge(aux_free, out_of(("f", 0)))
                    mm(bank[:, 0:S], sw[:, 0, :], hT[:, :], start=True, stop=True)
                    mm(bank[:, P:P + S], sw[:, 1, :], hT[:, :], start=True, stop=True)
                    t = mm(bank[0:S, 2 * P:3 * P], hT[:, :], sw[:, 2, :], start=True, stop=True)
                elif n < 6:
                    if n == 2:
                        pe.wait_ge(aux_free, out_of(("f", 1)))
                    t = mm(bank[0:S, 0:GW], qT[:, :], kbd[:, 4 * (n - 2):4 * (n - 1), :].rearrange("p a s -> p (a s)"),
                           start=True, stop=True)
                elif n < 10:
                    pe.wait_ge(exp_out, b * 4 + (n - 5))
                    for k in range(4):
                        t = tr(bank[0:S, k * S:(k + 1) * S], ex[:, n - 6, k, :], ident[0:S, 0:S])
                elif n == 10:
                    pe.wait_ge(pt_out, b * 4 + 4)
                    for h in range(H):
                        t = mm(bank[0:S, h * (DS + 1):(h + 1) * (DS + 1)], pT[:, h // 4, (h % 4) * S:(h % 4 + 1) * S],
                               v9[:, h, :], start=True, stop=True)
                elif n == 11:
                    pe.wait_ge(aux_free, out_of(("f", 10)))
                    t = tr(bank[:, 0:S], sctx[:, :, :].rearrange("p h d -> p (h d)"), ident[0:S, 0:S])
                elif n == 12:
                    pe.wait_ge(aux_free, out_of(("f", 11)))
                    t = mm(bank[0:S, 0:D], sctxT[:, :], sw[:, 3, :], start=True, stop=True)
                else:
                    pe.wait_ge(f_step, f_at(b, "h2"))
                    t = tr(bank[:, 0:S], hn2[:, :], ident[0:S, 0:S])
                t.then_inc(aux_full, 1)

            run_aux(aux, PREP, 0, "prep", 0)

            def body(b, kind, parity):
                for i in range(UNITS):
                    score_unit(b, parity, i)
                    one, two, three = steps(kind)[0][i]
                    run_aux(aux, one, b, kind, parity)

                    def middle():
                        run_aux(aux, two, b, kind, parity)

                    if i >= 2:
                        pv_unit(b, parity, i - 2, middle)
                    elif kind != "first":
                        pv_unit(b - 1, 1 - parity, UNITS - 2 + i, middle)
                    else:
                        middle()
                    run_aux(aux, three, b, kind, parity)

            batches(pe, body)
            for i in (UNITS - 2, UNITS - 1):
                pv_unit(B - 1, 1, i)
            run_aux(aux, LAST, B, "end", 0)

            def group(q):
                for n in range(EU + LAG):
                    if n < EU:
                        gate_up(q, n)
                    if n >= LAG:
                        down(q, n - LAG)

            groups(pe, group, lambda: pe.wait_ge(h_lo_out, 2))

        @block.scalar
        def _(act):
            a = nc.scalar.activation
            act.wait_ge(x_in, 16 * X_LOADS)
            a(tx[:, :], gx[:, :], ACT.Tanh).then_inc(set_act, 1)
            a(tf[:, :], gf[:, :], ACT.Tanh).then_inc(set_act, 1)
            set_wait(act, set_pe, SET_PE, "wkT")
            a(wkT[:, :, :].rearrange("p (a k) c -> p a (k c)", a=2), psum[:, 2:4, 0:4 * C], ACT.Copy).then_inc(set_act, 1)
            set_wait(act, set_pe, SET_PE, "wvT")
            a(wvT[:, :, :].rearrange("p (a k) c -> p a (k c)", a=2), psum[:, 4:6, 0:4 * C], ACT.Copy).then_inc(set_act, 1)
            set_wait(act, set_pe, SET_PE, "Mh")
            for k in range(2):
                ins = a(Mh_r[:, 1, 4 * k:4 * k + 4, :], psum[:, 2 + k, 0:4 * C].rearrange("p (k c) -> p k c", c=C),
                        ACT.Copy)
            ins.then_inc(set_act, 1)

            def evac_hi(seq, par, unit, parity):
                kind, n = unit
                act.wait_ge(aux_full, seq + 1)
                if kind == "t":
                    w = min(512, KV - 512 * n)
                    a(cT_hi[parity][0:C, 512 * n:512 * n + w], psum[0:C, AUXB + par, 0:w], ACT.Copy).then_inc(hi_out, 1)
                else:
                    a(qk_hi[parity][0:C, GW * n:GW * (n + 1)], psum[0:C, AUXB + par, 0:GW], ACT.Copy).then_inc(hi_out, 1)

            def ctx_hi_parts(b, kind, parity):
                act.wait_ge(ctx_in, (b + 1) * 32)
                if kind not in ("prep", "first"):
                    act.wait_ge(pv, (b - 1) * UNITS)
                for r, js in CTX_PARTS:
                    ins = a(c_hi[parity][0:r, js, 0:C], ctx_nat[0:r, js, :], ACT.Copy)
                ins.then_inc(ctx_hi, 1)

            def probs(b, i):
                m = kc(i % CH)[1]
                act.wait_ge(scores, b * UNITS + (i + 1))
                if not (isinstance(b, int) and b == 0 and i < 3):
                    act.wait_ge(*lo_made(b, i - 3))
                    act.wait_ge(pv, b * UNITS + (i - 2))
                src = psum[0:m, 2 * (i % 2):2 * (i % 2) + 2, 0:GW]
                a(p32[0:m, i % 3, :, :], src, ACT.Exp, scale=DH ** -0.5)
                a(p_hi[0:m, i % 3, :, :], src, ACT.Exp, scale=DH ** -0.5).then_inc(probs_hi, 1)

            def acc_evac(b, half):
                act.wait_ge(pv, b * UNITS + (half + 1) * CH)
                a(acc_sb[half][:, :, :], psum[0:C + 1, ACCB:ACCB + 2, 0:GW], ACT.Copy).then_inc(acc_out, 1)

            def self_exp(free, c, g):
                act.wait_ge(aux_free, free + 1)
                a(ex[:, g, :, :], ex[:, g, :, :], ACT.Exp, scale=DS ** -0.5).then_inc(exp_out, 1)

            def hidden_hi(q, n):
                act.wait_ge(hid, q * EU + (n + 1))
                wait_past(act, down_full, q * EU + max(n - (HS - 1), 0))
                a(hid_hi[:, n % HS, :], hidden[:, n % 3, :], ACT.Copy).then_inc(hid_hi_out, 1)

            def silu_unit(q, n):
                act.wait_ge(gu_full, q * EU + (n + 1))
                wait_past(act, hid, q * EU + max(n - 2, 0))
                a(silu[:, n % 3, :], psum[:, 2 * (n % 2), 0:GW], ACT.Silu).then_inc(silu_out, 1)

            def router_exp_step(part, n):
                if n in RT_EXPS:
                    act.wait_ge(top, part * len(ROUTER) + (ROUTER.index(RT_EXPS[n]) + 1))
                    bs = slice(*PARTS[part])
                    t = rt_p[:, bs, :] if RT_EXPS[n] == "sub" else rt_e[:, bs]
                    a(t, t, ACT.Exp).then_inc(router_exp, 1)

            def aux(seq, free, par, unit, b, parity, out_of, last):
                if unit[0] in ("t", "q"):
                    evac_hi(seq, par, unit, parity)
                elif unit[0] == "f" and 2 <= unit[1] < 6:
                    self_exp(free, b, unit[1] - 2)
                elif unit[0] == "r":
                    cols = part_cols(unit[1])
                    act.wait_ge(aux_free, free)
                    a(h_hi[:, cols], h2T[:, cols], ACT.Copy).then_inc(h_hi_out, 1)
                elif unit[0] == "rt":
                    router_exp_step(0, unit[1])
                elif unit[0] == "e":
                    if unit[1] < EU:
                        silu_unit(0, unit[1])
                    if 0 <= unit[1] - 2 < EU:
                        hidden_hi(0, unit[1] - 2)
                elif by_act(unit):
                    act.wait_ge(aux_full, seq + 1)
                    a(pT[:, unit[1] - 6, :], psum[0:S, AUXB + par, 0:GW], ACT.Copy).then_inc(pt_out, 1)

            set_wait(act, set_pool, SET_POOL, "pad c_lo1")
            ctx_hi_parts(0, "prep", 0)
            run_aux(aux, PREP, 0, "prep", 0)

            def body(b, kind, parity):
                for i in range(UNITS):
                    if i == CTX_AT and kind != "last":
                        ctx_hi_parts(b + 1, kind, 1 - parity)
                    probs(b, i)
                    if i == 2 and kind not in ("first", "last"):
                        act.wait_ge(scores, b * UNITS)
                    for third in steps(kind)[0][i]:
                        run_aux(aux, third, b, kind, parity)
                    if i == 1 and kind != "first":
                        acc_evac(b - 1, 1)
                    if i == CH + 1:
                        acc_evac(b, 0)

            batches(act, body)
            acc_evac(B - 1, 1)
            run_aux(aux, LAST, B, "end", 0)

            def group(q):
                for n in range(EU + 1):
                    if n < EU:
                        silu_unit(q, n)
                    if n:
                        hidden_hi(q, n - 1)
                    if isinstance(q, int) and q == 1 and n < RT_UNITS:
                        router_exp_step(1, n)

            groups(act, group)

        @block.vector
        def _(dve):
            v = nc.vector
            tt, ts, stt, cp = v.tensor_tensor, v.tensor_scalar, v.scalar_tensor_tensor, v.tensor_copy

            def step(name, ins, wait=True):
                ins.then_inc(set_dve, 1)
                if wait:
                    set_wait(dve, set_dve, SET_DVE, name)

            def layernorm(n, part):
                bs = cut(n, 4)
                xg, cg, sq = x1[:, bs, :], xc[:, bs, :], sqb[:, bs, :]

                def per_token(t):
                    return t[:, bs].unsqueeze(2).broadcast_to([S, 4, D])

                if part == "a":
                    step(f"sum{n}", v.tensor_reduce(lnsum[:, bs], xg, AX.X, ALU.add))
                    step(f"mean{n}", ts(lnsum[:, bs], lnsum[:, bs], 1.0 / D, None, ALU.mult))
                    step(f"centred{n}", tt(cg, xg, per_token(lnsum), ALU.subtract))
                elif part == "b":
                    step(f"square{n}", tt(sq, cg, cg, ALU.mult))
                    step(f"sumsq{n}", v.tensor_reduce(lnvar[:, bs], sq, AX.X, ALU.add))
                    step(f"lnvar{n}", ts(lnvar[:, bs], lnvar[:, bs], 1.0 / D, LN_EPS, ALU.mult, ALU.add))
                else:
                    set_wait(dve, set_pool, SET_POOL, f"lnr{n}")
                    step(f"xln{n}", tt(cg, cg, per_token(lnr), ALU.mult))

            dve.wait_ge(x_in, 16 * X_LOADS)
            layernorm(0, "a")
            layernorm(0, "b")
            set_wait(dve, set_pe, SET_PE, "wqT")
            step("wqT", cp(wqT[:, :, :].rearrange("p (a k) d -> p a (k d)", a=2), psum[:, 0:2, :]))
            layernorm(0, "c")
            set_wait(dve, set_act, SET_ACT, "tx")
            step("bot", ts(bot[:, :], bo[:, :], tx[0:S, 0:1], None, ALU.mult))
            set_wait(dve, set_pe, SET_PE, "xlnT0")
            step("xlnT0", cp(xlnT[:, 0:GW], psum[:, AUXB, 0:GW]))
            set_wait(dve, set_pe, SET_PE, "Mh")
            for k in range(2):
                ins = cp(Mh_r[:, 0, 4 * k:4 * k + 4, :], psum[:, k, 0:4 * C].rearrange("p (k c) -> p k c", c=C))
            step("Mh0", ins)

            set_wait(dve, set_pool, SET_POOL, "head_mask")

            def split_weights(k, n):
                es = slice(n // 2 * 3, n // 2 * 3 + 3)
                w = (wg, wu, wd_flat)[k][:, es, :]
                hi, lo = w_hi[k][:, es, :], w_lo[k][:, es, :]
                done = k * NW_PARTS + n
                if n % 2 == 0:
                    ins = ts(hi, w, n2[:, 0:1], None, ALU.mult) if k < 2 else cp(hi, w)
                else:
                    dve.wait_ge(w_split, done)
                    ins = stt(lo, w, n2[:, 0:1], hi, ALU.mult, ALU.subtract) if k < 2 else \
                        tt(lo, w, hi, ALU.subtract)
                ins.then_inc(w_split, 1)

            def f_inc(ins, c, name, wait=False):
                ins.then_inc(f_step, 1)
                if wait:
                    wait_apart(dve, f_step, f_at(c, name))

            def router(part, unit):
                b0, b1 = PARTS[part]
                bs, nb = slice(b0, b1), b1 - b0

                def be(t):
                    return t.unsqueeze(2).broadcast_to([S, nb, E])

                p, most = rt_p[:, bs, :], rt_m[:, bs]
                rank = rt_no[:, :].unsqueeze(1).broadcast_to([S, nb, E])
                for k in range(RT_CUTS[unit], RT_CUTS[unit + 1]):
                    name = ROUTER[k]
                    dve.wait_ge(top, part * len(ROUTER) + k) if part or k else None
                    if name in ("sum", "norm"):
                        dve.wait_ge(router_exp, 2 * part + (1 if name == "sum" else 2))
                    s = int(name[-1]) if name[-1] in "01" else 0
                    pick = rt_s[s][:, bs, :]
                    best = (rt_a, rt_b)[s][:, bs]
                    ins = {
                        "max": lambda: v.tensor_reduce(most, p, AX.X, ALU.max),
                        "sub": lambda: tt(p, p, be(most), ALU.subtract),
                        "sum": lambda: v.tensor_reduce(most, p, AX.X, ALU.add),
                        "inv": lambda: v.reciprocal(most, most),
                        "prob": lambda: tt(p, p, be(most), ALU.mult),
                        "best": lambda: v.tensor_reduce(best, p, AX.X, ALU.max),
                        "tie": lambda: tt(pick, p, be(best), ALU.is_equal),
                        "rank": lambda: tt(pick, pick, rank, ALU.mult),
                        "first": lambda: v.tensor_reduce(most, pick, AX.X, ALU.max),
                        "pick": lambda: tt(pick, rank, be(most), ALU.is_equal),
                        "drop": lambda: stt(p, pick, -2.0, p, ALU.mult, ALU.add),
                        "gap": lambda: tt(rt_e[:, bs], rt_b[:, bs], rt_a[:, bs], ALU.subtract),
                        "norm": lambda: ts(most, rt_e[:, bs], 1.0, None, ALU.add),
                        "weight0": lambda: v.reciprocal(rt_a[:, bs], most),
                        "weight1": lambda: tt(rt_b[:, bs], rt_a[:, bs], rt_e[:, bs], ALU.mult),
                        "weigh": lambda: tt(pick, pick, be(best), ALU.mult),
                        "add": lambda: tt(comb[:, bs, 0:E], rt_s[0][:, bs, :], rt_s[1][:, bs, :], ALU.add),
                        "shared": lambda: v.memset(comb[:, bs, E:E + 1], 1.0),
                    }
                    ins = ins.get(name) or ins[name[:-1]]
                    ins().then_inc(top, 1)

            def hidden_unit(q, n):
                dve.wait_ge(silu_out, q * EU + (n + 1))
                wait_past(dve, hid_lo_out, q * EU + max(n - 2, 0))
                tt(hidden[:, n % 3, :], silu[:, n % 3, :], psum[:, 2 * (n % 2) + 1, 0:GW], ALU.mult).then_inc(hid, 1)

            def add_expert(q, e):
                dve.wait_ge(down_full, q * EU + NF * (e + 1))
                if e:
                    dve.wait_ge(sum2, q * 4 * (E + 1) + 4 * e)
                for k in range(4):
                    xb = x2[:, bat(q * 4 + k), :].squeeze(1)
                    w = comb[:, bat(q * 4 + k), e]
                    stt(xb, psum[0:S, ACCB + e % 2, k * D:(k + 1) * D], w, xb, ALU.mult, ALU.add).then_inc(sum2, 1)

            def result(q):
                dve.wait_ge(sum2, (q + 1) * 4 * (E + 1))
                four = cut(q, 4)
                stt(sqb[:, four, :], x2[:, four, :], tf[0:S, 0:1], x1[:, four, :], ALU.mult, ALU.add).then_inc(fin, 1)

            def aux(seq, free, par, unit, b, parity, out_of, last):
                kind, n = unit
                bank = psum[:, AUXB + par, :]
                if kind == "ln":
                    wait_apart(dve, y_add, (b + 1) * 2 * HALF)
                    f_inc(v.bn_stats(stats[:, :], x1[:, bat(b), :]), b, "stats", True)
                    f_inc(v.bn_aggr(aggr[:, :], stats[:, :]), b, "aggr", True)
                    return
                if kind == "xf":
                    dve.wait_ge(pool_step, p_at(b, "rr"))
                    f_inc(ts(xf[:, :], x1[:, bat(b), :].squeeze(1), aggr[:, 0:1], pcol("rstd"),
                             ALU.subtract, ALU.mult), b, "xf")
                    f_inc(ts(hn[:, :], x1[:, bat(b), :].squeeze(1), aggr[:, 0:1], pcol("rr"),
                             ALU.subtract, ALU.mult), b, "h", True)
                    return
                if kind == "rs":
                    wait_apart(dve, aux_free, free)
                    f_inc(v.bn_stats(stats2[:, :], x2[:, bat(b), :]), b, "stats2", True)
                    f_inc(v.bn_aggr(aggr2[:, :], stats2[:, :]), b, "aggr2", True)
                    return
                if kind == "h2":
                    dve.wait_ge(pool_step, p_at(b, "r2"))
                    f_inc(ts(hn2[:, :], x2[:, bat(b), :].squeeze(1), pcol("r2"), None, ALU.mult), b, "h2")
                    return
                if kind in ("t", "q"):
                    dve.wait_ge(hi_out, b * 7 + (n + 1 + 3 * (kind == "q")))
                    if kind == "t":
                        cols = slice(512 * n, min(KV, 512 * (n + 1)))
                        hi, lo = cT_hi[parity][0:C, cols], cT_lo[parity][:, cols]
                        w = cols.stop - cols.start
                    else:
                        w = GW
                        hi, lo = (t[parity][0:C, GW * n:GW * (n + 1)] for t in (qk_hi, qk_lo))
                    tt(lo, bank[0:C, 0:w], hi, ALU.subtract).then_inc(aux_free, 1)
                    return
                if kind == "rt":
                    router(0, n)
                    return
                if kind in ("la", "lb", "lc"):
                    if n == 1 and kind == "la":
                        dve.wait_ge(w_in, 16 * W_LOADS)
                    layernorm(n, kind[1])
                    return
                if kind == "x1":
                    xg = x1[:, cut(n, 4), :]
                    step(f"x1 {n}", tt(xg, xg, bot[:, :].unsqueeze(1).broadcast_to([S, 4, D]), ALU.add))
                    return
                if kind == "e":
                    if 0 <= n - 1 < EU:
                        hidden_unit(0, n - 1)
                    if n >= 5 and n % 2 == 1:
                        add_expert(0, (n - 5) // 2)
                    if n == EU + 3:
                        result(0)
                    return
                if by_act(unit):
                    return
                dve.wait_ge(aux_full, seq + 1)
                if kind == "x":
                    cp(xlnT[:, cut(n, GW)], bank[:, 0:GW]).then_inc(aux_free, 1)
                    return
                if kind == "nh":
                    ts(Nh_r[:, n // 2, 4 * (n % 2):4 * (n % 2) + 4, 0:D], bank[0:C, :].rearrange("p (k c) -> p k c", c=D),
                       tx[0:C, 0:1], None, ALU.mult).then_inc(aux_free, 1)
                    return
                if kind == "r":
                    cp(rt_p[:, slice(*PARTS[n]), :], bank[0:S, 0:B * E].rearrange("p (b e) -> p b e", e=E)
                       [:, slice(*PARTS[n]), :]).then_inc(aux_free, 1)
                    dve.wait_ge(aux_free, free + 1)
                    return
                if kind == "p":
                    rt, part = divmod(n, MP)
                    w = min(MW, KV - part * MW)
                    r = rows_of(rt)
                    v.tensor_reduce(mx[0:r, rt, part:part + 1], bank[0:r, 0:w], AX.X, ALU.max)\
                        .then_inc(aux_free, 1)
                    if n == NPU - 1:
                        dve.wait_ge(aux_free, free + 1)
                        v.tensor_reduce(mx_row[:, :], mx[:, :, :], AX.X, ALU.max).then_inc(max_step, 1)
                        dve.wait_ge(max_step, b * 2 + 1)
                        ts(mneg[:, :], mx_row[:, :], -1.0, SHIFT, ALU.mult, ALU.add).then_inc(max_step, 1)
                elif kind == "m":
                    if not (isinstance(b, int) and b == 0):
                        dve.wait_ge(row_in, b * 32)
                    cp(mrow[:, :], bank[0:RT, 0:P // 2].bitcast(F16)).then_inc(aux_free, 1)
                elif kind in ("y0", "y1"):
                    half = int(kind[1])
                    nh = len(YB[n])
                    heads = bank[0:S, 0:nh * YW].rearrange("p (k w) -> p k w", w=YW)
                    at = half * len(YB) + n
                    dve.wait_ge(aux_free, free)
                    v.reciprocal(y_rc[:, 0:nh], heads[:, :, D]).then_inc(y_rcp, 1)
                    if not (isinstance(b, int) and b == 0 and at < 2):
                        dve.wait_ge(y_add, b * 2 * HALF + (Y_READ[at - 2] - 2 * HALF * (at < 2)))
                    dve.wait_ge(y_rcp, b * 2 * len(YB) + (at + 1))
                    tt(y_sb[:, at % 2, 0:nh, :], heads[:, :, 0:D],
                       y_rc[:, 0:nh].unsqueeze(2).broadcast_to([S, nh, D]), ALU.mult).then_inc(aux_free, 1)
                elif n == 0:
                    cp(hT[:, :], bank[:, 0:S]).then_inc(aux_free, 1)
                elif n == 1:
                    f_inc(cp(qT[:, :], bank[:, 0:S]), b, "qT")
                    f_inc(cp(v9[:, :, 0:DS], bank[0:S, 2 * P:3 * P].rearrange("p (h d) -> p h d", d=DS)), b, "v")
                    tt(kbd[:, :, :], bank[:, P:P + S].unsqueeze(1).broadcast_to([P, H, S]),
                       head_mask[:, :].unsqueeze(2).broadcast_to([P, H, S]), ALU.mult).then_inc(aux_free, 1)
                elif n < 6:
                    g = n - 2
                    sc = bank[0:S, 0:GW].rearrange("p (k s) -> p k s", s=S)
                    f_inc(v.tensor_reduce(mx4[:, g, :], sc, AX.X, ALU.max), b, f"mx{g}", True)
                    tt(ex[:, g, :, :], sc, mx4[:, g, :].unsqueeze(2).broadcast_to([S, 4, S]),
                       ALU.subtract).then_inc(aux_free, 1)
                elif n == 10:
                    o9 = bank[0:S, 0:H * (DS + 1)].rearrange("p (h d) -> p h d", d=DS + 1)
                    f_inc(v.reciprocal(s_rc[:, :], o9[:, :, DS]), b, "rc", True)
                    tt(sctx[:, :, :], o9[:, :, 0:DS], s_rc[:, :].unsqueeze(2).broadcast_to([S, H, DS]),
                       ALU.mult).then_inc(aux_free, 1)
                elif n == 11:
                    cp(sctxT[:, :], bank[:, 0:S]).then_inc(aux_free, 1)
                elif n == 12:
                    tt(x2[:, bat(b), :].squeeze(1), bank[0:S, 0:D], xf[:, :], ALU.add).then_inc(aux_free, 1)
                else:
                    cp(h2T[:, tok(b)], bank[:, 0:S]).then_inc(aux_free, 1)

            run_aux(aux, PREP, 0, "prep", 0)

            def body(b, kind, parity):
                for i in range(UNITS):
                    one, two, three = steps(kind)[0][i]
                    run_aux(aux, one, b, kind, parity)
                    if i and i - 1 not in LO_POOL:
                        probs_rest(dve, v, b, i - 1)
                    elif not i and kind != "first":
                        probs_rest(dve, v, b - 1, UNITS - 1)
                    run_aux(aux, two, b, kind, parity)
                    if kind == "last" and 0 <= i - 4 < 3 * NW_PARTS:
                        if i == 4:
                            dve.wait_ge(e_in, 16 * E_LOADS)
                        split_weights(*divmod(i - 4, NW_PARTS))
                    run_aux(aux, three, b, kind, parity)

            batches(dve, body)
            probs_rest(dve, v, B - 1, UNITS - 1)
            run_aux(aux, LAST, B, "end", 0)

            def group(q):
                for n in range(EU):
                    hidden_unit(q, n)
                    if n >= 5 and n % 2 == 1:
                        add_expert(q, (n - 5) // 2)
                    if isinstance(q, int) and q == 1 and n < RT_UNITS:
                        router(1, n)
                for e in (E - 1, E):
                    add_expert(q, e)
                result(q)

            groups(dve, group)


_INS = ["x", "ctx_768", "g_xattn", "g_ffn", "L0_xattn_w_q", "L0_xattn_w_k", "L0_xattn_w_v", "L0_xattn_w_o",
        "L0_xattn_b_o", "L0_ffn_norm1_w", "L0_ffn_norm2_w", "L0_ffn_wq", "L0_ffn_wk", "L0_ffn_wv", "L0_ffn_wo",
        "L0_ffn_router_w", "L0_ffn_sh_gate", "L0_ffn_sh_up", "L0_ffn_sh_down", "L0_ffn_e_gate", "L0_ffn_e_up",
        "L0_ffn_e_down"]
_OUTS = [((16, 100, 128), "float32")]


def kernel(**inputs):
    import numpy as _np
    import concourse.bacc as _bacc
    from concourse import mybir as _mybir
    from concourse.bass_utils import run_bass_kernel_spmd as _run

    nc = _bacc.Bacc("TRN2", target_bir_lowering=False, num_devices=1)
    arrays, args = {}, []
    for name in _INS:
        a = _np.ascontiguousarray(inputs[name])
        arrays[f"in_{name}_dram"] = a
        args.append(nc.dram_tensor(f"in_{name}_dram", a.shape, _mybir.dt.from_np(a.dtype), kind="ExternalInput").ap())
    for i, (shape, dtype) in enumerate(_OUTS):
        dt = _mybir.dt.from_np(_np.dtype(dtype))
        args.append(nc.dram_tensor(f"out_{i}_dram", shape, dt, kind="ExternalOutput").ap())
    flamingo_kernel(nc, *args)
    r = _run(nc, [arrays], core_ids=[0])
    return r.results[0]["out_0_dram"]
```
